# Optimizing a Trainium2 kernel written in Bass

```python
import numpy as np
import jax
import jax.numpy as jnp

def _softmax(x, axis=-1):
    return jax.nn.softmax(x, axis=axis)

def _gelu(x):
    return jax.nn.gelu(x, approximate=True)

def _silu(x):
    return jax.nn.silu(x)

def _sigmoid(x):
    return jax.nn.sigmoid(x)

def _layernorm(x, axis=-1, eps=1e-05):
    m = jnp.mean(x, axis=axis, keepdims=True)
    v = jnp.var(x, axis=axis, keepdims=True)
    return (x - m) / jnp.sqrt(v + eps)

def _scatter_add(tgt, idx, src, axis=0):
    return tgt.at[idx].add(src)

def _segment_sum(src, seg, n):
    return jax.ops.segment_sum(src, seg, n)
kernel_name = 'mk_decoder_preln_d1_seqx_r8_791d06'

def setup_inputs(seed: int=0):
    np.random.seed(seed)
    _w = jnp.asarray

    def _rec_inputs():
        import jax
        import jax.numpy as jnp
        _rk = jax.random.key(seed)
        x = -0.000929 + 1 * jax.random.normal(jax.random.fold_in(_rk, 1), (64, 128, 128), jnp.float32)
        _lenS = 128 - jax.random.randint(jax.random.fold_in(_rk, 7), (64,), 0, max(1, 128 // 4) + 1, jnp.int32)
        _lenS2 = 77 - jax.random.randint(jax.random.fold_in(_rk, 8), (64,), 0, max(1, 77 // 4) + 1, jnp.int32)
        _ctx_1024P = jax.random.normal(jax.random.fold_in(_rk, 11), (64, 16, 128), jnp.float32)
        _ctx_1024c = jax.random.dirichlet(jax.random.fold_in(_rk, 511), 0.3 * jnp.ones((16,), jnp.float32), (64, 77))
        _ctx_1024t = jnp.einsum('bsk,bkd->bsd', _ctx_1024c, _ctx_1024P)
        _ctx_1024t = _ctx_1024t * jax.lax.rsqrt(jnp.mean(jnp.square(_ctx_1024t)) + 1e-12) * 0.953939
        ctx_1024 = -1.52775e-05 + 0.999936 * (_ctx_1024t + 0.3 * jax.random.normal(jax.random.fold_in(_rk, 611), (64, 77, 128), jnp.float32))
        return (x, ctx_1024)
    x, ctx_1024 = _rec_inputs()

    def _L0_attn_setup():
        import jax, jax.numpy as jnp
        import numpy as np
        DIM = 128
        NUM_HEADS = 16
        HEAD_DIM = 64
        EPS = 1e-06

        def _feature_map(x, proj):
            return jax.nn.elu(x @ proj) + 1.0
        key = jax.random.key(seed)
        ks = jax.random.split(key, 6)
        x = jax.random.normal(ks[0], (4, 256, DIM), dtype=jnp.float32)
        Wq = jax.random.normal(ks[1], (DIM, NUM_HEADS * HEAD_DIM), dtype=jnp.float32) / np.sqrt(DIM)
        Wk = jax.random.normal(ks[2], (DIM, NUM_HEADS * HEAD_DIM), dtype=jnp.float32) / np.sqrt(DIM)
        Wv = jax.random.normal(ks[3], (DIM, NUM_HEADS * HEAD_DIM), dtype=jnp.float32) / np.sqrt(DIM)
        Wo = jax.random.normal(ks[4], (NUM_HEADS * HEAD_DIM, DIM), dtype=jnp.float32) / np.sqrt(NUM_HEADS * HEAD_DIM)
        proj = jax.random.normal(ks[5], (HEAD_DIM, HEAD_DIM), dtype=jnp.float32) / np.sqrt(HEAD_DIM)
        return {'x': x, 'Wq': Wq, 'Wk': Wk, 'Wv': Wv, 'Wo': Wo, 'proj': proj}
    _L0_attn_all = _L0_attn_setup()
    _L0_attn_in = {k: v for k, v in _L0_attn_all.items() if k in ('Wq', 'Wk', 'Wv', 'Wo', 'proj')}
    del _L0_attn_all

    def _L0_xattn_setup():
        import jax, jax.numpy as jnp
        import numpy as np
        DIM = 128
        H = 16
        D = 64
        INNER = H * D
        EPS = 1e-05

        def layernorm(x, w, b):
            mu = jnp.mean(x, axis=-1, keepdims=True)
            var = jnp.var(x, axis=-1, keepdims=True)
            return (x - mu) * jax.lax.rsqrt(var + EPS) * w + b
        key = jax.random.key(seed)
        ks = jax.random.split(key, 8)
        B, N, S = (4, 32, 1024)
        s = 1.0 / np.sqrt(DIM)
        return {'latents': jax.random.normal(ks[0], (B, N, DIM), jnp.float32), 'context': jax.random.normal(ks[1], (B, S, DIM), jnp.float32), 'ln_l_w': jnp.ones((DIM,), jnp.float32), 'ln_l_b': jnp.zeros((DIM,), jnp.float32), 'ln_c_w': jnp.ones((DIM,), jnp.float32), 'ln_c_b': jnp.zeros((DIM,), jnp.float32), 'Wq': jax.random.normal(ks[2], (DIM, INNER), jnp.float32) * s, 'Wkv': jax.random.normal(ks[3], (DIM, 2 * INNER), jnp.float32) * s, 'Wo': jax.random.normal(ks[4], (INNER, DIM), jnp.float32) * (1.0 / np.sqrt(INNER)), 'bo': jnp.zeros((DIM,), jnp.float32)}
    _L0_xattn_all = _L0_xattn_setup()
    _L0_xattn_in = {k: v for k, v in _L0_xattn_all.items() if k in ('ln_l_w', 'ln_l_b', 'ln_c_w', 'ln_c_b', 'Wq', 'Wkv', 'Wo', 'bo')}
    del _L0_xattn_all

    def _L0_ffn_setup():
        import jax, jax.numpy as jnp
        import numpy as np
        key = jax.random.key(seed)
        kx, kw = jax.random.split(key)
        x = jax.random.normal(kx, (32, 512, 128), dtype=jnp.float32)
        weight = jax.random.normal(kw, (128, 128), dtype=jnp.float32) * 0.01
        return {'x': x, 'weight': weight}
    _L0_ffn_all = _L0_ffn_setup()
    _L0_ffn_in = {k: v for k, v in _L0_ffn_all.items() if k in ('weight',)}
    del _L0_ffn_all
    return {'x': x, 'ctx_1024': ctx_1024, 'L0_attn_Wq': _L0_attn_in['Wq'], 'L0_attn_Wk': _L0_attn_in['Wk'], 'L0_attn_Wv': _L0_attn_in['Wv'], 'L0_attn_Wo': _L0_attn_in['Wo'], 'L0_attn_proj': _L0_attn_in['proj'], 'L0_xattn_ln_l_w': _L0_xattn_in['ln_l_w'], 'L0_xattn_ln_l_b': _L0_xattn_in['ln_l_b'], 'L0_xattn_ln_c_w': _L0_xattn_in['ln_c_w'], 'L0_xattn_ln_c_b': _L0_xattn_in['ln_c_b'], 'L0_xattn_Wq': _L0_xattn_in['Wq'], 'L0_xattn_Wkv': _L0_xattn_in['Wkv'], 'L0_xattn_Wo': _L0_xattn_in['Wo'], 'L0_xattn_bo': _L0_xattn_in['bo'], 'L0_ffn_weight': _L0_ffn_in['weight']}

def reference(x, ctx_1024, L0_attn_Wq, L0_attn_Wk, L0_attn_Wv, L0_attn_Wo, L0_attn_proj, L0_xattn_ln_l_w, L0_xattn_ln_l_b, L0_xattn_ln_c_w, L0_xattn_ln_c_b, L0_xattn_Wq, L0_xattn_Wkv, L0_xattn_Wo, L0_xattn_bo, L0_ffn_weight):
    import jax
    import jax.numpy as jnp

    def _L0_attn_ref(x, Wq, Wk, Wv, Wo, proj):
        import jax, jax.numpy as jnp
        import numpy as np
        DIM = 128
        NUM_HEADS = 16
        HEAD_DIM = 64
        EPS = 1e-06

        def _feature_map(x, proj):
            return jax.nn.elu(x @ proj) + 1.0
        B, S, _ = x.shape
        H, D = (NUM_HEADS, HEAD_DIM)
        q = (x @ Wq).reshape(B, S, H, D)
        k = (x @ Wk).reshape(B, S, H, D)
        v = (x @ Wv).reshape(B, S, H, D)
        q = _feature_map(q, proj)
        k = _feature_map(k, proj)
        q_t = jnp.moveaxis(q, 1, 0)
        k_t = jnp.moveaxis(k, 1, 0)
        v_t = jnp.moveaxis(v, 1, 0)

        def step(carry, qkv):
            kv, ksum = carry
            qt, kt, vt = qkv
            kv = kv + kt[..., :, None] * vt[..., None, :]
            ksum = ksum + kt
            num = jnp.einsum('bhd,bhde->bhe', qt, kv)
            den = jnp.einsum('bhd,bhd->bh', qt, ksum) + EPS
            return ((kv, ksum), num / den[..., None])
        kv0 = jnp.zeros((B, H, D, D), dtype=x.dtype)
        ks0 = jnp.zeros((B, H, D), dtype=x.dtype)
        _, out = jax.lax.scan(step, (kv0, ks0), (q_t, k_t, v_t))
        out = jnp.moveaxis(out, 0, 1).reshape(B, S, H * D)
        return out @ Wo

    def _L0_xattn_ref(latents, context, ln_l_w, ln_l_b, ln_c_w, ln_c_b, Wq, Wkv, Wo, bo):
        import jax, jax.numpy as jnp
        import numpy as np
        DIM = 128
        H = 16
        D = 64
        INNER = H * D
        EPS = 1e-05

        def layernorm(x, w, b):
            mu = jnp.mean(x, axis=-1, keepdims=True)
            var = jnp.var(x, axis=-1, keepdims=True)
            return (x - mu) * jax.lax.rsqrt(var + EPS) * w + b
        b, n, _ = latents.shape
        s = context.shape[1]
        lat = layernorm(latents, ln_l_w, ln_l_b)
        ctx = layernorm(context, ln_c_w, ln_c_b)
        q = (lat @ Wq).reshape(b, n, H, D).transpose(0, 2, 1, 3)
        kv = ctx @ Wkv
        k, v = jnp.split(kv, 2, axis=-1)
        k = k.reshape(b, s, H, D).transpose(0, 2, 1, 3)
        v = v.reshape(b, s, H, D).transpose(0, 2, 1, 3)
        scale = D ** (-0.5)
        attn = jnp.einsum('bhnd,bhsd->bhns', q, k) * scale
        attn = jnp.clip(attn, -11.0, 11.0)
        attn = jax.nn.softmax(attn, axis=-1)
        out = jnp.einsum('bhns,bhsd->bhnd', attn, v)
        out = out.transpose(0, 2, 1, 3).reshape(b, n, INNER)
        return out @ Wo + bo

    def _L0_ffn_ref(x, weight):
        import jax, jax.numpy as jnp
        import numpy as np
        b_weight = jnp.sign(weight)
        return jnp.einsum('bsi,oi->bso', x, b_weight)
    x = x + _L0_attn_ref(_layernorm(x, axis=-1), L0_attn_Wq, L0_attn_Wk, L0_attn_Wv, L0_attn_Wo, L0_attn_proj)
    x = x + _L0_xattn_ref(_layernorm(x, axis=-1), ctx_1024, L0_xattn_ln_l_w, L0_xattn_ln_l_b, L0_xattn_ln_c_w, L0_xattn_ln_c_b, L0_xattn_Wq, L0_xattn_Wkv, L0_xattn_Wo, L0_xattn_bo)
    x = x + _L0_ffn_ref(_layernorm(x, axis=-1), L0_ffn_weight)
    return x

_drawn_inputs = setup_inputs


def setup_inputs(seed=0):
    import zlib

    import numpy as np

    out = dict(_drawn_inputs(seed))
    spreads = {'L0_xattn_ln_l_w': (1.0, 0.2),
     'L0_xattn_ln_l_b': (0.0, 0.428),
     'L0_xattn_ln_c_w': (1.0, 0.2),
     'L0_xattn_ln_c_b': (0.0, 0.1),
     'L0_xattn_bo': (0.0, 0.1)}
    factors = {'L0_attn_Wq': 4.439, 'L0_attn_Wk': 2.989, 'L0_attn_proj': 3.34}
    for name, (base, spread) in spreads.items():
        noise = np.random.default_rng([zlib.crc32(name.encode()), seed]).standard_normal(out[name].shape)
        drawn = base * np.exp(spread * noise) if base else spread * noise
        out[name] = jnp.asarray(drawn.astype(out[name].dtype))
    for name, factor in factors.items():
        out[name] = (out[name] * factor).astype(out[name].dtype)
    return out
```

```python
import concourse.bass as bass
from concourse import mybir
from contextlib import ExitStack


def decoder_layer(nc, x, ctx_in, wq1, wk1, wv1, wo1, proj, lnl_w, lnl_b, lnc_w, lnc_b,
                  wq2, wkv2, wo2, bo2, w_ffn, out):
    F32 = mybir.dt.float32
    F32R = mybir.dt.float32r
    ALU = mybir.AluOpType
    ACT = mybir.ActivationFunctionType
    AX = mybir.AxisListType

    NB, S, D = x.shape
    C = ctx_in.shape[1]
    HD = proj.shape[0]
    NH = wq1.shape[1] // HD
    NP = NH // 2
    GB = 4
    NG = NB // GB
    W = GB * S
    GC = GB * C
    INNER = NH * HD
    HALF = INNER // 2
    QH = 4
    NQ = NH // QH
    QC = QH * C
    EPS_OUT = 1e-5
    EPS_LN = 1e-5
    EPS_DEN = 1e-6
    SCALE = float(HD) ** -0.5
    EXP_HI, EXP_LO = 59874.141715197817, 1.670170079024566e-05

    stack = ExitStack()
    with stack:
        def sb(name, shape, dt=F32):
            return stack.enter_context(nc.sbuf_tensor(name, shape, dt))

        def sem(name):
            return stack.enter_context(nc.semaphore(name))

        X = sb("X", [128, NB, D])
        CX = sb("CX", [C, NB, D])
        ident = sb("ident", [128, 128])
        causal = sb("causal", [128, 1, S])
        wq1_hi, wq1_lo = sb("wq1_hi", [D, INNER], F32R), sb("wq1_lo", [D, INNER], F32R)
        wk1_hi, wk1_lo = sb("wk1_hi", [D, INNER], F32R), sb("wk1_lo", [D, INNER], F32R)
        wv1_hi, wv1_lo = sb("wv1_hi", [D, INNER], F32R), sb("wv1_lo", [D, INNER], F32R)
        wv2_hi, wv2_lo = sb("wv2_hi", [D, INNER], F32R), sb("wv2_lo", [D, INNER], F32R)
        m_hi, m_lo = sb("m_hi", [D, NH, D], F32R), sb("m_lo", [D, NH, D], F32R)
        wo1_sb = sb("wo1_sb", [128, NP, D])
        wo2_sb = sb("wo2_sb", [128, NP, D])
        sign_t = sb("sign_t", [D, D], F32R)
        lnl_w_sb, lnl_b_sb = sb("lnl_w_sb", [D, 1]), sb("lnl_b_sb", [D, 1])
        lnc_w_sb, lnc_b_sb = sb("lnc_w_sb", [D, 1]), sb("lnc_b_sb", [D, 1])
        bo_sb = sb("bo_sb", [D, 1])

        st6 = sb("st6", [128, GB, 6])
        mean = sb("mean", [128, GB, 1])
        m_sum, m_dif = sb("m_sum", [128, GB]), sb("m_dif", [128, GB])
        sq_sum, sq_dif = sb("sq_sum", [128, GB]), sb("sq_dif", [128, GB])
        var_part = sb("var_part", [128, GB])
        r1 = sb("r1", [128, GB, 1])
        r2 = sb("r2", [128, GB, 1])
        t1 = sb("t1", [128, GB, 1])
        minus_half = sb("minus_half", [128, 16])

        def variance(dve, parts, n, a, b, halves, done):
            p = slice(0, parts)
            dve.tensor_tensor(m_sum[p], st6[p, :, 1], st6[p, :, 4], ALU.add)
            dve.tensor_tensor(m_dif[p], st6[p, :, 1], st6[p, :, 4], ALU.subtract)
            dve.tensor_tensor(sq_sum[p], st6[p, :, 2], st6[p, :, 5], ALU.add).then_inc(halves, 1)
            dve.wait_ge(halves, 2 * n + 1)
            dve.tensor_scalar(mean[p, :, 0], m_sum[p], 0.5, None, ALU.mult)
            dve.tensor_scalar(var_part[p], sq_sum[p], a / D, b, ALU.mult, ALU.add)
            dve.scalar_tensor_tensor(sq_dif[p], m_dif[p], a / 4, m_dif[p], ALU.mult, ALU.mult).then_inc(halves, 1)
            dve.wait_ge(halves, 2 * n + 2)
            dve.tensor_tensor(t1[p, :, 0], var_part[p], sq_dif[p], ALU.add).then_inc(done, 1)

        PS = stack.enter_context(nc.psum_tensor("PS", [128, 8, 512], F32))

        w_loaded = sem("w_loaded")
        wv_loaded = sem("wv_loaded")
        x_in = [sem(f"x_in{i}") for i in range(3)]
        ctx_loaded = sem("ctx_loaded")
        zeroed, consts = sem("zeroed"), sem("consts")
        prep_mm, prep_cp, prep_hi, prep_lo = sem("prep_mm"), sem("prep_cp"), sem("prep_hi"), sem("prep_lo")
        wv_hi_done, wv_done, sign_done = sem("wv_hi_done"), sem("wv_done"), sem("sign_done")
        sign_gt, sign_lt = sem("sign_gt"), sem("sign_lt")
        x_cut = [0, GB, 4 * GB, NB] if NB > 4 * GB else [0, GB, 2 * GB, NB]

        prep_stack = ExitStack()
        with prep_stack:
            def psb(name, shape, dt=F32):
                return prep_stack.enter_context(nc.sbuf_tensor(name, shape, dt))

            raw = [psb(f"raw{i}", [D, INNER]) for i in range(4)]
            rawv = [psb(f"rawv{i}", [D, INNER]) for i in range(2)]
            wt = [psb(f"wt{i}", [128, INNER]) for i in range(4)]
            projbd = psb("projbd", [128, 128])
            ffn_raw, ffn_gt, ffn_lt = psb("ffn_raw", [D, D]), psb("ffn_gt", [D, D]), psb("ffn_lt", [D, D])
            NT = 4 * NP // 4
            NC = 2 * (2 * NP // 8)
            NM = NH // 4
            with nc.Block() as block:

                @block.sync
                def _(sp):
                    for i, src in enumerate([wq1, wk1, wq2]):
                        sp.dma_start(raw[i][:], src).then_inc(w_loaded, 16)
                    sp.dma_start(raw[3][:], wkv2[:, 0:INNER]).then_inc(w_loaded, 16)
                    for c in range(2):
                        sp.dma_start(X[:, x_cut[c]:x_cut[c + 1], :],
                                     x[x_cut[c]:x_cut[c + 1]].rearrange("b s d -> s b d")).then_inc(x_in[c], 16)
                    sp.dma_start(X[:, x_cut[2]:NB, :],
                                 x[x_cut[2]:NB].rearrange("b s d -> s b d")).then_inc(x_in[2], 16)
                    sp.dma_start(CX[:], ctx_in.rearrange("b c d -> c b d")).then_inc(ctx_loaded, 16)

                @block.gpsimd
                def _(pool):
                    pool.memset(projbd[:], 0.0).then_inc(zeroed, 1)
                    pool.memset(ident[:], 0.0).then_inc(zeroed, 1)
                    pool.memset(causal[:], 1.0).then_inc(zeroed, 1)
                    pool.memset(minus_half[:], -0.5).then_inc(zeroed, 1)
                    pool.wait_ge(zeroed, 4)
                    pool.affine_select(out=ident[:], in_=ident[:], compare_op=ALU.not_equal, fill=1.0,
                                       base=0, pattern=[[-1, 128]], channel_multiplier=1).then_inc(consts, 1)
                    pool.affine_select(out=causal[:, 0, :], in_=causal[:, 0, :], compare_op=ALU.is_ge, fill=0.0,
                                       base=0, pattern=[[1, S]], channel_multiplier=-1).then_inc(consts, 1)

                @block.tensor
                def _(pe):
                    pe.wait_ge(consts, 2)
                    pe.wait_ge(w_loaded, 13 * 16)
                    bank = [0]

                    def next_bank():
                        if bank[0] >= 2:
                            pe.wait_ge(prep_cp, bank[0] - 1)
                        b = PS[:, bank[0] % 2, :]
                        bank[0] += 1
                        return b

                    for i in range(4):
                        for c in range(0, NP, 4):
                            b = next_bank()
                            for k in range(4):
                                at = (c + k) * 128
                                mm = pe.transpose(b[:, k * 128:(k + 1) * 128], raw[i][:, at:at + 128], ident[:])
                            mm.then_inc(prep_mm, 1)
                    pe.wait_ge(prep_cp, NT)
                    for i in range(2):
                        for c in range(0, NP, 4):
                            b = next_bank()
                            for k in range(4):
                                at = (c + k) * 128
                                mm = pe.matmul(b[:, k * 128:(k + 1) * 128], wt[i][:, at:at + 128], projbd[:],
                                               start=True, stop=True)
                            mm.then_inc(prep_mm, 1)
                    for c in range(0, NH, 4):
                        b = next_bank()
                        for k in range(4):
                            h = (c // 8) * 8 + (c // 4) % 2 + 2 * k
                            r, at = HD * (h % 2), (h // 2) * 128
                            mm = pe.matmul(b[:, k * 128:(k + 1) * 128], wt[3][r:r + HD, at:at + 128],
                                           wt[2][r:r + HD, at:at + 128], start=True, stop=True)
                        mm.then_inc(prep_mm, 1)
                    b = next_bank()
                    pe.transpose(b[:, 0:128], ffn_raw[:], ident[:]).then_inc(prep_mm, 1)

                dests = []
                for hi, lo in ((wq1_hi, wq1_lo), (wk1_hi, wk1_lo)):
                    for c in range(0, NP, 4):
                        dests.append((hi[:, c * 128:(c + 4) * 128], lo[:, c * 128:(c + 4) * 128]))
                for c in range(0, NH, 4):
                    h = (c // 8) * 8 + (c // 4) % 2
                    dests.append((m_hi[:, h:h + 7:2, :], m_lo[:, h:h + 7:2, :]))

                @block.scalar
                def _(act):
                    act.wait_ge(zeroed, 3)
                    act.dma_start(projbd[0:HD, 0:HD], proj).then_inc(w_loaded, 16)
                    act.dma_start(projbd[HD:128, HD:128], proj).then_inc(w_loaded, 16)
                    act.dma_start(ffn_raw[:], w_ffn).then_inc(w_loaded, 16)
                    for dst, src in ((lnl_w_sb, lnl_w), (lnl_b_sb, lnl_b), (lnc_w_sb, lnc_w), (lnc_b_sb, lnc_b),
                                     (bo_sb, bo2)):
                        act.dma_start(dst[:], src.rearrange("(d o) -> d o", o=1)).then_inc(w_loaded, 16)
                    act.dma_start(wo1_sb[:], wo1.rearrange("(p r) d -> r p d", r=128)).then_inc(w_loaded, 16)
                    act.dma_start(rawv[0][:], wv1).then_inc(wv_loaded, 16)
                    act.dma_start(rawv[1][:], wkv2[:, INNER:2 * INNER]).then_inc(wv_loaded, 16)
                    act.dma_start(wo2_sb[:], wo2.rearrange("(p r) d -> r p d", r=128)).then_inc(wv_loaded, 16)
                    for n in range(NT):
                        act.wait_ge(prep_mm, n + 1)
                        i, c = n // (NP // 4), n % (NP // 4)
                        act.activation(wt[i][:, c * 512:(c + 1) * 512], PS[:, n % 2, :], ACT.Copy).then_inc(prep_cp, 1)
                    for n, (hi, _) in enumerate(dests):
                        act.wait_ge(prep_mm, NT + n + 1)
                        act.activation(hi, PS[:, (NT + n) % 2, :], ACT.Copy).then_inc(prep_hi, 1)
                    act.wait_ge(wv_loaded, 48)
                    for i, hi in enumerate((wv1_hi, wv2_hi)):
                        act.activation(hi[:], rawv[i][:], ACT.Copy).then_inc(wv_hi_done, 1)

                @block.vector
                def _(dve):
                    for n, (hi, lo) in enumerate(dests):
                        dve.wait_ge(prep_hi, n + 1)
                        dve.tensor_tensor(lo, PS[:, (NT + n) % 2, :], hi.bitcast(F32), ALU.subtract).then_inc(prep_cp, 1)
                    dve.wait_ge(wv_loaded, 48)
                    for i, (hi, lo) in enumerate(((wv1_hi, wv1_lo), (wv2_hi, wv2_lo))):
                        dve.wait_ge(wv_hi_done, i + 1)
                        dve.tensor_tensor(lo[:], rawv[i][:], hi[:].bitcast(F32), ALU.subtract).then_inc(wv_done, 1)
                    last = NT + len(dests)
                    dve.wait_ge(prep_mm, last + 1)
                    dve.tensor_scalar(ffn_gt[:], PS[:, last % 2, 0:D], 0.0, None, ALU.is_gt).then_inc(sign_gt, 1)
                    dve.tensor_scalar(ffn_lt[:], PS[:, last % 2, 0:D], 0.0, None, ALU.is_lt).then_inc(sign_lt, 1)
                    dve.wait_ge(sign_gt, 1)
                    dve.wait_ge(sign_lt, 1)
                    dve.tensor_tensor(sign_t[:], ffn_gt[:], ffn_lt[:], ALU.subtract).then_inc(sign_done, 1)

        with ExitStack() as pa:
            def asb(name, shape, dt=F32):
                return pa.enter_context(nc.sbuf_tensor(name, shape, dt))

            def asem(name):
                return pa.enter_context(nc.semaphore(name))

            xn = asb("a_xn", [128, GB, D])
            xt_hi, xt_lo = asb("a_xt_hi", [D, W], F32R), asb("a_xt_lo", [D, W], F32R)
            xtn_hi, xtn_lo = asb("a_xtn_hi", [D, W], F32R), asb("a_xtn_lo", [D, W], F32R)
            e_q, e_k = asb("a_e_q", [128, W]), asb("a_e_k", [128, W])
            fq = asb("a_fq", [128, 2, W])
            fk = asb("a_fk", [128, 2, W])
            am = asb("a_am", [128, 2, 2, GB, S])
            v = asb("a_v", [128, GB, NH, HD + 1])
            den = asb("a_den", [128, 2, GB, 1])
            rden = asb("a_rden", [128, 2, GB, 1])
            on = asb("a_on", [128, 2, GB, 2, HD])
            ot = asb("a_ot", [128, 2, W])
            acc_sb = asb("a_acc_sb", [D, W])

            B_QK, B_MISC, B_A, B_O, B_OT, B_ACC = 0, 1, 2, 4, 6, 7

            q_proj, k_proj = asem("q_proj"), asem("k_proj")
            nq_done, nk_done = asem("nq_done"), asem("nk_done")
            eq_done, ek_done = asem("eq_done"), asem("ek_done")
            fq_done, fk_done = asem("fq_done"), asem("fk_done")
            a_done, mask_done = asem("a_done"), asem("mask_done")
            av_done, norm_done = asem("av_done"), asem("norm_done")
            den_done, rden_done = asem("den_done"), asem("rden_done")
            ot_done, ote_done, wo_done = asem("ot_done"), asem("ote_done"), asem("wo_done")
            v_mm = asem("v_mm")
            misc_free = asem("misc_free")
            acc_evac, fin_done = asem("acc_evac"), asem("fin_done")
            ln_st, ln_mv, ln_v = asem("ln_st"), asem("ln_mv"), asem("ln_v")
            ln_r, xn_ready = asem("ln_r"), asem("xn_ready")
            xt_done, xthi_done, cur_ready = asem("xt_done"), asem("xthi_done"), asem("cur_ready")
            ones_set = asem("ones_set")

            N_PRO = 1 + GB

            def use(g, first, p, kind):
                i = p + (1 if p > 3 else 0)
                if kind == "xt":
                    i = 4
                if not first and (p > 1 or kind == "fin"):
                    i += 1
                return (N_PRO if first else 2 * NP * 0 + 10 * g + 4) + (i if not (kind == "fin") else 2)

            def ln_group(dve, g, n):
                for b in range(GB):
                    i = dve.bn_stats(st6[:, b, :], X[:, g * GB + b, :])
                i.then_inc(ln_st, 1)
                dve.wait_ge(ln_st, n + 1)
                variance(dve, 128, n, 1.0, EPS_OUT, ln_mv, ln_v)
                dve.wait_ge(ln_r, n + 1)
                for b in range(GB):
                    i = dve.tensor_scalar(xn[:, b, :], X[:, g * GB + b, :], mean[:, b, :], r1[:, b, :],
                                          ALU.subtract, ALU.mult)
                i.then_inc(xn_ready, 1)

            def split3(pe, dst, w_hi, w_lo, x_hi, x_lo):
                pe.matmul(dst, w_hi, x_hi, start=True, stop=False)
                pe.matmul(dst, w_hi, x_lo, start=False, stop=False)
                return pe.matmul(dst, w_lo, x_hi, start=False, stop=True)

            def v_args(b, half, hi, lo):
                s, c = slice(b * S, (b + 1) * S), slice(half * HALF, (half + 1) * HALF)
                return hi[:, s], lo[:, s], wv1_hi[:, c], wv1_lo[:, c]

            with nc.Block() as block:

                @block.sync
                def _(sp):
                    sp.wait_ge(x_in[2], 16)

                @block.tensor
                def _(pe):
                    def xt_transposes(g, i):
                        pe.wait_ge(xn_ready, g + 1)
                        if not (isinstance(i, int) and i == 0):
                            pe.wait_ge(misc_free, i)
                        for b in range(GB):
                            mm = pe.transpose(PS[:, B_MISC, b * S:(b + 1) * S], xn[:, b, :], ident[:])
                        mm.then_inc(xt_done, 1)

                    def v_half(b, half, hi, lo, i):
                        pe.wait_ge(misc_free, i)
                        split3(pe, PS[:, B_MISC, :], *v_args(b, half, hi, lo)).then_inc(v_mm, 1)

                    def proj_step(p, w_hi, w_lo, hi, lo, done):
                        c = slice(p * 128, (p + 1) * 128)
                        split3(pe, PS[:, B_QK, :], w_hi[:, c], w_lo[:, c], hi[:], lo[:]).then_inc(done, 1)

                    def transposes_and_v0():
                        pe.wait_ge(wv_done, 2)
                        xt_transposes(0, 0)
                        for b in range(GB):
                            v_half(b, 0, xtn_hi, xtn_lo, 1 + b)

                    def wo_step(p):
                        mm = pe.matmul(PS[:, B_ACC, :], wo1_sb[:, p, :], ot[:, p % 2, :],
                                       start=(p == 0), stop=(p == NP - 1))
                        mm.then_inc(wo_done, 1)

                    def fin_transposes(i, n):
                        pe.wait_ge(acc_evac, n)
                        pe.wait_ge(misc_free, i)
                        for b in range(GB):
                            mm = pe.transpose(PS[:, B_MISC, b * S:(b + 1) * S], acc_sb[:, b * S:(b + 1) * S], ident[:])
                        mm.then_inc(fin_done, 1)

                    def ot_transposes(p):
                        for b in range(GB):
                            mm = pe.transpose(PS[:, B_OT, b * S:(b + 1) * S],
                                              on[:, p % 2, b, :, :].rearrange("s h d -> s (h d)"), ident[:])
                        mm.then_inc(ot_done, 1)

                    def group(g, first, last):
                        for p in range(NP):
                            u = NP * g + p
                            begin = first and p == 0
                            more = not (last and p == NP - 1)
                            nxt = (p + 1) % NP
                            hi, lo = (xtn_hi, xtn_lo) if p == NP - 1 else (xt_hi, xt_lo)
                            if more:
                                if p == 0:
                                    pe.wait_ge(cur_ready, g + 1)
                                if p == NP - 1:
                                    pe.wait_ge(misc_free, use(g, first, 3, "xt") + 1)
                                pe.wait_ge(fk_done, u + 1)
                                proj_step(nxt, wq1_hi, wq1_lo, hi, lo, q_proj)
                            pe.wait_ge(fq_done, u + 1)
                            pe.wait_ge(fk_done, u + 1)
                            for h in range(2):
                                if not begin:
                                    pe.wait_ge(mask_done, 2 * u - 1 + h)
                                for b in range(GB):
                                    r = slice(h * HD, (h + 1) * HD)
                                    c = slice(b * S, (b + 1) * S)
                                    mm = pe.matmul(PS[:, B_A + h, c], fk[r, p % 2, c], fq[r, p % 2, c],
                                                   start=True, stop=True)
                                mm.then_inc(a_done, 1)
                            if not begin:
                                pe.wait_ge(norm_done, u)
                                if not (first and p == 1):
                                    pe.wait_ge(ote_done, u - 1)
                                ot_transposes((p - 1) % NP)
                            if more:
                                pe.wait_ge(fq_done, u + 2)
                                proj_step(nxt, wk1_hi, wk1_lo, hi, lo, k_proj)
                            if p < GB:
                                v_half(p, 1, xt_hi, xt_lo, use(g, first, p, "v"))
                            elif not last:
                                v_half(p - GB, 0, xtn_hi, xtn_lo, use(g, first, p, "v"))
                            if p == 0:
                                pe.wait_ge(misc_free, use(g, first, 0, "v"))
                            if p == GB:
                                pe.wait_ge(misc_free, use(g, first, 3, "v") + 1)
                            for h in range(2):
                                pe.wait_ge(mask_done, 2 * u + 1 + h)
                                for b in range(GB):
                                    mm = pe.matmul(PS[:, B_O + h, b * (HD + 1):(b + 1) * (HD + 1)],
                                                   am[:, p % 2, h, b, :], v[:, b, 2 * p + h, :], start=True, stop=True)
                            mm.then_inc(av_done, 1)
                            if not begin:
                                pe.wait_ge(ote_done, u)
                                if p == 1 and not first:
                                    pe.wait_ge(acc_evac, g)
                                wo_step((p - 1) % NP)
                            if p == 1 and not first:
                                fin_transposes(use(g, first, 1, "fin"), g)
                            if p == 3 and not last:
                                xt_transposes(g + 1, use(g, first, 3, "xt"))

                    transposes_and_v0()
                    proj_step(0, wq1_hi, wq1_lo, xtn_hi, xtn_lo, q_proj)
                    pe.wait_ge(fq_done, 1)
                    proj_step(0, wk1_hi, wk1_lo, xtn_hi, xtn_lo, k_proj)
                    group(0, True, False)
                    with pe.Fori(1, NG - 1) as g:
                        group(g, False, False)
                    group(NG - 1, False, True)
                    U = NP * NG
                    pe.wait_ge(norm_done, U)
                    pe.wait_ge(ote_done, U - 1)
                    ot_transposes(NP - 1)
                    pe.wait_ge(ote_done, U)
                    wo_step(NP - 1)
                    fin_transposes(use(NG - 1, False, 3, "v") + 1, NG)

                @block.scalar
                def _(act):
                    def exp_step(u1, mm, e, read, negative, done):
                        act.wait_ge(mm, u1)
                        if read is not None:
                            act.wait_ge(*read)
                        act.activation(e[:], PS[:, B_QK, :], ACT.Relu, scale=-1.0).then_inc(negative, 1)
                        act.wait_ge(negative, u1)
                        act.activation(e[:], e[:], ACT.Exp, scale=-1.0).then_inc(done, 1)

                    def v_evac(b, half, n):
                        act.wait_ge(v_mm, n)
                        act.activation(v[:, b, half * NP:(half + 1) * NP, 0:HD],
                                       PS[:, B_MISC, :].rearrange("s (h d) -> s h d", d=HD),
                                       ACT.Copy).then_inc(misc_free, 1)

                    def ot_evac(p, n):
                        act.wait_ge(ot_done, n)
                        act.activation(ot[:, p % 2, :], PS[:, B_OT, :], ACT.Copy).then_inc(ote_done, 1)

                    def xt_hi_evac(n):
                        act.wait_ge(xt_done, n)
                        act.activation(xtn_hi[:], PS[:, B_MISC, :], ACT.Copy).then_inc(xthi_done, 1)

                    def copy_over():
                        act.activation(xt_hi[:], xtn_hi[:].bitcast(F32), ACT.Copy)
                        act.activation(xt_lo[:], xtn_lo[:].bitcast(F32), ACT.Copy).then_inc(cur_ready, 1)

                    def acc_to_sbuf(n):
                        act.wait_ge(wo_done, NP * n)
                        act.activation(acc_sb[:], PS[:, B_ACC, :], ACT.Copy).then_inc(acc_evac, 1)

                    def group(g, first, last):
                        for p in range(NP):
                            u = NP * g + p
                            begin = first and p == 0
                            more = not (last and p == NP - 1)
                            if more:
                                exp_step(u + 2, q_proj, e_q, (fq_done, u + 1), nq_done, eq_done)
                            if not begin:
                                if not (first and p < 3):
                                    act.wait_ge(wo_done, u - 2)
                                ot_evac((p - 1) % NP, u)
                            if p == 0 and not first:
                                acc_to_sbuf(g)
                            if more:
                                exp_step(u + 2, k_proj, e_k, (fk_done, u + 1), nk_done, ek_done)
                            if p < GB:
                                if not first:
                                    act.wait_ge(av_done, NP * g)
                                v_evac(p, 1, u + GB + 1)
                            elif not last:
                                act.wait_ge(av_done, u - p + NP // 2)
                                v_evac(p - GB, 0, u + GB + 1)
                            if p == 3 and not last:
                                xt_hi_evac(g + 2)
                            if p == NP - 1 and not last:
                                act.wait_ge(k_proj, u + 1)
                                act.wait_ge(misc_free, use(g, first, 3, "xt") + 1)
                                copy_over()

                    xt_hi_evac(1)
                    act.wait_ge(misc_free, 1)
                    copy_over()
                    for b in range(GB):
                        v_evac(b, 0, b + 1)
                    exp_step(1, q_proj, e_q, None, nq_done, eq_done)
                    exp_step(1, k_proj, e_k, None, nk_done, ek_done)
                    group(0, True, False)
                    with act.Fori(1, NG - 1) as g:
                        group(g, False, False)
                    group(NG - 1, False, True)
                    act.wait_ge(wo_done, NP * NG - 2)
                    ot_evac(NP - 1, NP * NG)
                    acc_to_sbuf(NG)

                @block.gpsimd
                def _(pool):
                    def factor(n):
                        pool.wait_ge(ln_v, n + 1)
                        pool.tensor_tensor(r1[:, :, 0], t1[:, :, 0], minus_half[:, 0:GB], ALU.pow).then_inc(ln_r, 1)

                    pool.memset(v[:, :, :, HD:HD + 1], 1.0).then_inc(ones_set, 1)
                    pool.wait_ge(zeroed, 4)
                    factor(0)
                    with pool.Fori(1, NG) as g:
                        factor(g)

                @block.vector
                def _(dve):
                    def feature(u1, par, e, ready, f, done):
                        dve.wait_ge(ready, u1)
                        dve.scalar_tensor_tensor(f[:, par, :], PS[:, B_QK, :], 0.0, e[:], ALU.max, ALU.add)\
                           .then_inc(done, 1)

                    def mask(p, h, n):
                        dve.wait_ge(a_done, n)
                        dve.tensor_tensor(am[:, p % 2, h], PS[:, B_A + h, :].rearrange("k (b s) -> k b s", s=S),
                                          causal[:].broadcast_to([128, GB, S]), ALU.mult).then_inc(mask_done, 1)

                    def normalise(p, n, wait_ot):
                        dve.wait_ge(av_done, n)
                        o = PS[:, B_O:B_O + 2, 0:GB * (HD + 1)].rearrange("s h (b e) -> s h b e", e=HD + 1)
                        dve.tensor_scalar(den[:, :, :, 0], o[:, :, :, HD], EPS_DEN, None, ALU.add).then_inc(den_done, 1)
                        dve.wait_ge(den_done, n)
                        dve.reciprocal(rden[:], den[:]).then_inc(rden_done, 1)
                        dve.wait_ge(rden_done, n)
                        if wait_ot is not None:
                            dve.wait_ge(ot_done, wait_ot)
                        dve.tensor_tensor(on[:, p % 2].rearrange("s b h d -> s h b d"), o[:, :, :, 0:HD],
                                          rden[:].broadcast_to([128, 2, GB, HD]), ALU.mult).then_inc(norm_done, 1)

                    def xt_lo_evac(n):
                        dve.wait_ge(xthi_done, n)
                        dve.tensor_tensor(xtn_lo[:], PS[:, B_MISC, :], xtn_hi[:].bitcast(F32), ALU.subtract)\
                           .then_inc(misc_free, 1)

                    def residual(g, n):
                        dve.wait_ge(fin_done, n)
                        xs = X[:, bass.ts(g, GB), :]
                        dve.tensor_tensor(xs, PS[:, B_MISC, :].rearrange("s (b d) -> s b d", d=D), xs, ALU.add)\
                           .then_inc(misc_free, 1)

                    def group(g, first, last):
                        for p in range(NP):
                            u = NP * g + p
                            begin = first and p == 0
                            more = not (last and p == NP - 1)
                            if not (first and p < 2):
                                dve.wait_ge(av_done, u - 1)
                            mask(p, 0, 2 * u + 1)
                            if more:
                                feature(u + 2, (p + 1) % 2, e_q, eq_done, fq, fq_done)
                            mask(p, 1, 2 * u + 2)
                            if p == 0 and not last:
                                if first:
                                    dve.wait_ge(x_in[1], 16)
                                ln_group(dve, g + 1, g + 1)
                            if p == 2 and not first:
                                residual(g - 1, g)
                            if more:
                                feature(u + 2, (p + 1) % 2, e_k, ek_done, fk, fk_done)
                            if p == 3 and not last:
                                pass
                            if p == 4 and not last:
                                xt_lo_evac(g + 2)
                            normalise(p, u + 1, None if first and p < 2 else u - 1)

                    dve.wait_ge(x_in[0], 16)
                    ln_group(dve, 0, 0)
                    xt_lo_evac(1)
                    dve.wait_ge(ones_set, 1)
                    feature(1, 0, e_q, eq_done, fq, fq_done)
                    feature(1, 0, e_k, ek_done, fk, fk_done)
                    group(0, True, False)
                    dve.wait_ge(x_in[2], 16)
                    with dve.Fori(1, NG - 1) as g:
                        group(g, False, False)
                    group(NG - 1, False, True)
                    residual(NG - 1, NG)

        with ExitStack() as pb:
            def bsb(name, shape, dt=F32):
                return pb.enter_context(nc.sbuf_tensor(name, shape, dt))

            def bsem(name):
                return pb.enter_context(nc.semaphore(name))

            cn = bsb("b_cn", [C, GB, D])
            cy = bsb("b_cy", [D, GC])
            ct_hi, ct_lo = bsb("b_ct_hi", [D, GC], F32R), bsb("b_ct_lo", [D, GC], F32R)
            ctn_hi, ctn_lo = bsb("b_ctn_hi", [D, GC], F32R), bsb("b_ctn_lo", [D, GC], F32R)
            ln_x = bsb("b_ln_x", [128, GB, D])
            lat_t = bsb("b_lat_t", [D, W])
            gs = bsb("b_gs", [D, 2, GB, QC])
            e = bsb("b_e", [128, 2, GB, QC])
            sums = bsb("b_sums", [128, GB * QH])
            rsum = bsb("b_rsum", [128, GB * QH, 1])
            pt = bsb("b_pt", [C, GB, QH, S])
            v2 = bsb("b_v2", [C, GB, NH, HD])
            ot2 = bsb("b_ot2", [128, 2, W])
            acc2_sb = bsb("b_acc_sb", [D, W])
            fn = bsb("b_fn", [128, GB, D])
            ft_hi, ft_lo = bsb("b_ft_hi", [D, W], F32R), bsb("b_ft_lo", [D, W], F32R)

            P_ACC, P_G, P_S, P_PT, P_MISC = 0, 1, 3, 5, 7

            g_mm, g_ev = bsem("g_mm"), bsem("g_ev")
            s_mm, s_ev = bsem("s_mm"), bsem("s_ev")
            clipped, summed, inverted, p_ready = bsem("clipped"), bsem("summed"), bsem("inverted"), bsem("p_ready")
            pt_mm, pt_ev = bsem("pt_mm"), bsem("pt_ev")
            pv_mm, ot_ev, wo_mm = bsem("pv_mm"), bsem("ot_ev"), bsem("wo_mm")
            v2_mm = bsem("v2_mm")
            misc2 = bsem("misc2")
            acc2_ev, fin2_mm = bsem("acc2_ev"), bsem("fin2_mm")
            st_done, mv_done, var_done, f_done = bsem("st_done"), bsem("mv_done"), bsem("var_done"), bsem("f_done")
            cn_ready, lnx_ready, fn_ready = bsem("cn_ready"), bsem("lnx_ready"), bsem("fn_ready")
            ct_mm, cthi_done, ctn_ready, ct_cur = bsem("ct_mm"), bsem("cthi_done"), bsem("ctn_ready"), bsem("ct_cur")
            lt_mm = bsem("lt_mm")
            ft_mm, fthi_done, ff_mm = bsem("ft_mm"), bsem("fthi_done"), bsem("ff_mm")
            x_out = bsem("x_out")

            M_PRO = 4

            def m_use(g, first, last, q, kind, i=0):
                order = []
                for qq in range(NQ):
                    if qq == 2 and not last:
                        order.append((qq, "ct", 0))
                    if qq == 3 and not first:
                        order.append((qq, "ft", 0))
                    if not (last and qq == 3):
                        order += [(qq, "v", 0), (qq, "v", 1)]
                    if qq == 1 and not first:
                        order.append((qq, "fin", 0))
                    if qq == 3 and not first:
                        order.append((qq, "ff", 0))
                    if qq == 3 and not last:
                        order.append((qq, "lt", 0))
                return (M_PRO if first else 13 * g + 1) + order.index((q, kind, i))

            M_END = 13 * (NG - 1) + 1 + 9

            def norm_factor(dve, src, parts, n, a, b):
                for k in range(GB):
                    i = dve.bn_stats(st6[0:parts, k, :], src(k))
                i.then_inc(st_done, 1)
                dve.wait_ge(st_done, n + 1)
                variance(dve, parts, n, a, b, mv_done, var_done)

            def norm_apply(dve, src, dst, parts, n, ready):
                dve.wait_ge(f_done, n + 1)
                for k in range(GB):
                    i = dve.tensor_scalar(dst[0:parts, k, :], src(k), mean[0:parts, k, :], r1[0:parts, k, :],
                                          ALU.subtract, ALU.mult)
                i.then_inc(ready, 1)

            with nc.Block() as block:

                @block.sync
                def _(sp):
                    def store(g, i):
                        sp.wait_ge(misc2, i + 1)
                        sp.dma_start(out[bass.ts(g, GB)].rearrange("b s d -> s b d"), X[:, bass.ts(g, GB), :])\
                          .then_inc(x_out, 16)

                    with sp.Fori(0, NG - 2) as g:
                        store(g, 13 * g + 25)
                    store(NG - 2, M_END - 1)
                    store(NG - 1, M_END + 2)
                    sp.wait_ge(x_out, 16 * NG)

                @block.gpsimd
                def _(pool):
                    with pool.Fori(0, 3 * NG) as n:
                        pool.wait_ge(var_done, n + 1)
                        pool.tensor_tensor(r1[:, :, 0], t1[:, :, 0], minus_half[:, 0:GB], ALU.pow).then_inc(f_done, 1)

                @block.tensor
                def _(pe):
                    def three(dst, w_hi, w_lo, x_hi, x_lo):
                        pe.matmul(dst, w_hi, x_hi, start=True, stop=False)
                        pe.matmul(dst, w_hi, x_lo, start=False, stop=False)
                        return pe.matmul(dst, w_lo, x_hi, start=False, stop=True)

                    def g_step(q, hi, lo, base):
                        for i in range(QH):
                            h = QH * q + i
                            if not (isinstance(base, int) and base + i < 2):
                                pe.wait_ge(g_ev, base + i - 1)
                            three(PS[:, P_G + i % 2, 0:GC], m_hi[:, h, :], m_lo[:, h, :], hi[:], lo[:]).then_inc(g_mm, 1)

                    def v_step(b, half, hi, lo, i):
                        pe.wait_ge(misc2, i)
                        s, c = slice(b * C, (b + 1) * C), slice(half * HALF, (half + 1) * HALF)
                        three(PS[0:C, P_MISC, :], hi[:, s], lo[:, s], wv2_hi[:, c], wv2_lo[:, c]).then_inc(v2_mm, 1)

                    def four_transposes(src, done):
                        for b in range(GB):
                            mm = pe.transpose(PS[:, P_MISC, b * S:(b + 1) * S], src(b), ident[:])
                        mm.then_inc(done, 1)

                    def ct_transposes(n, i):
                        pe.wait_ge(cn_ready, n)
                        if i is not None:
                            pe.wait_ge(misc2, i)
                        for b in range(GB):
                            mm = pe.transpose(PS[:, P_MISC, b * C:(b + 1) * C], cn[:, b, :], ident[0:C, 0:C])
                        mm.then_inc(ct_mm, 1)

                    def lt_transposes(n, i):
                        pe.wait_ge(lnx_ready, n)
                        pe.wait_ge(misc2, i)
                        four_transposes(lambda b: ln_x[:, b, :], lt_mm)

                    def fin_transposes(n, i):
                        pe.wait_ge(acc2_ev, n)
                        pe.wait_ge(misc2, i)
                        four_transposes(lambda b: acc2_sb[:, b * S:(b + 1) * S], fin2_mm)

                    def ft_transposes(n, i):
                        pe.wait_ge(fn_ready, n)
                        pe.wait_ge(misc2, i)
                        four_transposes(lambda b: fn[:, b, :], ft_mm)

                    def ffn(i_ft, i):
                        pe.wait_ge(misc2, i_ft + 1)
                        pe.wait_ge(misc2, i)
                        for b in range(GB):
                            s = slice(b * S, (b + 1) * S)
                            pe.matmul(PS[:, P_MISC, s], ft_hi[:, s], sign_t[:], start=True, stop=False)
                            mm = pe.matmul(PS[:, P_MISC, s], ft_lo[:, s], sign_t[:], start=False, stop=True)
                        mm.then_inc(ff_mm, 1)

                    def wo_step(q, n):
                        pe.wait_ge(ot_ev, n)
                        for pp in range(2):
                            k = 2 * q + pp
                            mm = pe.matmul(PS[:, P_ACC, :], wo2_sb[:, k, :], ot2[:, pp, :],
                                           start=(k == 0), stop=(k == NP - 1))
                        mm.then_inc(wo_mm, 1)

                    def scores(q, u, begin):
                        pe.wait_ge(g_ev, QH * (u + 1))
                        for b in range(GB):
                            if b < 2 and not begin:
                                pe.wait_ge(ot_ev, 2 * (u - 2) + b + 1)
                            elif b >= 2 or not (isinstance(u, int) and u == 0):
                                pe.wait_ge(s_ev, GB * u + b - 1)
                            pe.matmul(PS[:, P_S + b % 2, 0:QC], lat_t[:, b * S:(b + 1) * S], gs[:, q % 2, b, :],
                                      start=True, stop=True).then_inc(s_mm, 1)

                    def pt_step(q, v, begin):
                        pe.wait_ge(p_ready, v + 1)
                        for b in range(GB):
                            if not (begin and b < 2):
                                pe.wait_ge(pt_ev, GB * v + b - 1)
                            for i in range(QH):
                                mm = pe.transpose(PS[0:C, P_PT + b % 2, i * S:(i + 1) * S],
                                                  e[:, q % 2, b, i * C:(i + 1) * C], ident[:])
                            mm.then_inc(pt_mm, 1)

                    def pv_step(q, v, exps):
                        pe.wait_ge(s_ev, exps)
                        pe.wait_ge(pt_ev, GB * (v + 1))
                        for pp in range(2):
                            for b in range(GB):
                                for i in range(2):
                                    mm = pe.matmul(PS[i * HD:(i + 1) * HD, P_S + pp, b * S:(b + 1) * S],
                                                   v2[:, b, QH * q + 2 * pp + i, :], pt[:, b, 2 * pp + i, :],
                                                   start=True, stop=True)
                            mm.then_inc(pv_mm, 1)

                    def group(g, first, last):
                        for q in range(NQ):
                            u = NQ * g + q
                            more = not (last and q == NQ - 1)

                            def at(kind, i=0):
                                return m_use(g, first, last, q, kind, i)
                            if more:
                                if q == 0:
                                    pe.wait_ge(ct_cur, g + 1)
                                if q == NQ - 1:
                                    pe.wait_ge(ctn_ready, g + 2)
                                hi, lo = (ctn_hi, ctn_lo) if q == NQ - 1 else (ct_hi, ct_lo)
                                g_step((q + 1) % NQ, hi, lo, QH * (u + 1))
                            if not (first and q < 2):
                                if q == 2 and not first:
                                    pe.wait_ge(acc2_ev, g)
                                wo_step((q - 2) % NQ, 2 * (u - 1))
                            if q == 0:
                                pe.wait_ge(misc2, 2 if first else 13 * g + 1)
                            scores(q, u, first and q < 2)
                            if q == 2 and not last:
                                ct_transposes(g + 2, at("ct"))
                            if q == 3 and not first:
                                ft_transposes(g, at("ft"))
                            if not (first and q == 0):
                                pt_step((q - 1) % NQ, u - 1, first and q == 1)
                            if q == 0:
                                v_step(2, 0, ct_hi, ct_lo, at("v", 0))
                                v_step(3, 0, ct_hi, ct_lo, at("v", 1))
                            elif q < 3:
                                v_step(2 * q - 2, 1, ct_hi, ct_lo, at("v", 0))
                                v_step(2 * q - 1, 1, ct_hi, ct_lo, at("v", 1))
                            elif not last:
                                v_step(0, 0, ctn_hi, ctn_lo, at("v", 0))
                                v_step(1, 0, ctn_hi, ctn_lo, at("v", 1))
                            if not (first and q == 0):
                                if q == 1:
                                    pe.wait_ge(misc2, m_use(g, first, last, 0, "v", 1) + 1)
                                if q == 3:
                                    pe.wait_ge(misc2, m_use(g, first, last, 2, "v", 1) + 1)
                                pv_step((q - 1) % NQ, u - 1, GB * (u + 1))
                            if q == 1 and not first:
                                fin_transposes(g, at("fin"))
                            if q == 3 and not first:
                                ffn(m_use(g, first, last, 3, "ft"), at("ff"))
                            if q == 3 and not last:
                                lt_transposes(g + 2, at("lt"))

                    pe.wait_ge(consts, 2)
                    ct_transposes(1, None)
                    lt_transposes(1, 1)
                    pe.wait_ge(ctn_ready, 1)
                    v_step(0, 0, ctn_hi, ctn_lo, 2)
                    v_step(1, 0, ctn_hi, ctn_lo, 3)
                    g_step(0, ctn_hi, ctn_lo, 0)
                    group(0, True, False)
                    with pe.Fori(1, NG - 1) as g:
                        group(g, False, False)
                    group(NG - 1, False, True)
                    U = NQ * NG
                    wo_step(NQ - 2, 2 * (U - 1))
                    pt_step(NQ - 1, U - 1, False)
                    pv_step(NQ - 1, U - 1, GB * U)
                    wo_step(NQ - 1, 2 * U)
                    fin_transposes(NG, M_END)
                    ft_transposes(NG, M_END + 1)
                    ffn(M_END + 1, M_END + 2)

                @block.scalar
                def _(act):
                    def copy(dst, src, done):
                        act.activation(dst, src, ACT.Copy).then_inc(done, 1)

                    def ct_hi_step(i):
                        act.wait_ge(misc2, i + 1)
                        copy(ctn_hi[:], cy[:], cthi_done)

                    def copy_over():
                        act.activation(ct_hi[:], ctn_hi[:].bitcast(F32), ACT.Copy)
                        copy(ct_lo[:], ctn_lo[:].bitcast(F32), ct_cur)

                    def v_ev(b, half, n):
                        act.wait_ge(v2_mm, n)
                        copy(v2[:, b, half * NP:(half + 1) * NP, :],
                             PS[0:C, P_MISC, :].rearrange("c (h d) -> c h d", d=HD), misc2)

                    def exp_step(q, u):
                        for b in range(GB):
                            act.wait_ge(s_mm, GB * u + b + 1)
                            act.activation(e[:, q % 2, b, :], PS[:, P_S + b % 2, 0:QC], ACT.Exp, scale=SCALE)\
                               .then_inc(s_ev, 1)

                    def pt_ev_step(v):
                        for b in range(GB):
                            act.wait_ge(pt_mm, GB * v + b + 1)
                            copy(pt[:, b], PS[0:C, P_PT + b % 2, :].rearrange("c (h s) -> c h s", s=S), pt_ev)

                    def ot_ev_step(v):
                        for pp in range(2):
                            act.wait_ge(pv_mm, 2 * v + pp + 1)
                            copy(ot2[:, pp, :], PS[:, P_S + pp, :], ot_ev)

                    def acc_ev_step(n):
                        act.wait_ge(wo_mm, NQ * n)
                        act.activation(acc2_sb[:], PS[:, P_ACC, :], ACT.Identity, bias=bo_sb[:]).then_inc(acc2_ev, 1)

                    def ft_hi_step(n):
                        act.wait_ge(ft_mm, n)
                        copy(ft_hi[:], PS[:, P_MISC, :], fthi_done)

                    def group(g, first, last):
                        for q in range(NQ):
                            u = NQ * g + q
                            if q == 1 and not first:
                                acc_ev_step(g)
                            if not (first and q < 2):
                                act.wait_ge(pt_mm, GB * (u - 1))
                            exp_step(q, u)
                            if q == 3 and not first:
                                ft_hi_step(g)
                            if not (first and q == 0):
                                pt_ev_step(u - 1)
                            n = 2 * u + 2
                            if q == 0:
                                v_ev(2, 0, n + 1)
                                v_ev(3, 0, n + 2)
                            elif q < 3:
                                if q == 1 and not first:
                                    act.wait_ge(pv_mm, 2 * NQ * g)
                                v_ev(2 * q - 2, 1, n + 1)
                                v_ev(2 * q - 1, 1, n + 2)
                            elif not last:
                                act.wait_ge(pv_mm, 2 * (u - 1))
                                v_ev(0, 0, n + 1)
                                v_ev(1, 0, n + 2)
                            if q == 2 and not last:
                                ct_hi_step(m_use(g, first, last, 2, "ct"))
                            if q == 3 and not last:
                                act.wait_ge(ctn_ready, g + 2)
                                copy_over()
                            if not (first and q == 0):
                                ot_ev_step(u - 1)

                    ct_hi_step(0)
                    act.wait_ge(ctn_ready, 1)
                    copy_over()
                    v_ev(0, 0, 1)
                    v_ev(1, 0, 2)
                    group(0, True, False)
                    with act.Fori(1, NG - 1) as g:
                        group(g, False, False)
                    group(NG - 1, False, True)
                    pt_ev_step(NQ * NG - 1)
                    ot_ev_step(NQ * NG - 1)
                    acc_ev_step(NG)
                    ft_hi_step(NG)

                @block.vector
                def _(dve):
                    A2, B2 = 1.0 + EPS_LN, EPS_OUT * EPS_LN

                    def x_of(g):
                        return lambda k: X[:, g * GB + k, :]

                    def c_of(g):
                        return lambda k: CX[:, g * GB + k, :]

                    def norm_ctx(g, n):
                        norm_factor(dve, c_of(g), C, n, 1.0, EPS_LN)
                        norm_apply(dve, c_of(g), cn, C, n, cn_ready)

                    def norm_lat(g, n):
                        norm_factor(dve, x_of(g), 128, n, A2, B2)
                        norm_apply(dve, x_of(g), ln_x, 128, n, lnx_ready)

                    def norm_ffn(g, n):
                        norm_factor(dve, x_of(g), 128, n, 1.0, EPS_OUT)
                        norm_apply(dve, x_of(g), fn, 128, n, fn_ready)

                    def cy_step(n):
                        dve.wait_ge(ct_mm, n)
                        dve.tensor_scalar(cy[:], PS[:, P_MISC, 0:GC], lnc_w_sb[:], lnc_b_sb[:], ALU.mult, ALU.add)\
                           .then_inc(misc2, 1)

                    def ct_lo_step(n):
                        dve.wait_ge(cthi_done, n)
                        dve.tensor_tensor(ctn_lo[:], cy[:], ctn_hi[:].bitcast(F32), ALU.subtract).then_inc(ctn_ready, 1)

                    def lat_step(n):
                        dve.wait_ge(lt_mm, n)
                        dve.tensor_scalar(lat_t[:], PS[:, P_MISC, :], lnl_w_sb[:], lnl_b_sb[:], ALU.mult, ALU.add)\
                           .then_inc(misc2, 1)

                    def g_ev_step(q, base):
                        for i in range(QH):
                            dve.wait_ge(g_mm, base + i + 1)
                            dve.tensor_copy(gs[:, q % 2, :, i * C:(i + 1) * C],
                                            PS[:, P_G + i % 2, 0:GC].rearrange("p (b c) -> p b c", c=C)).then_inc(g_ev, 1)

                    def softmax(q, u):
                        flat = e[:, q % 2].rearrange("s b c -> s (b c)")
                        rows = flat.rearrange("s (r c) -> s r c", c=C)
                        dve.wait_ge(s_ev, GB * (u + 1))
                        dve.tensor_scalar(flat, flat, EXP_HI, EXP_LO, ALU.min, ALU.max).then_inc(clipped, 1)
                        dve.wait_ge(clipped, u + 1)
                        dve.reduce_sum(sums[:], rows, AX.X).then_inc(summed, 1)
                        dve.wait_ge(summed, u + 1)
                        dve.reciprocal(rsum[:, :, 0], sums[:]).then_inc(inverted, 1)
                        dve.wait_ge(inverted, u + 1)
                        dve.tensor_tensor(rows, rows, rsum[:].broadcast_to([128, GB * QH, C]), ALU.mult)\
                           .then_inc(p_ready, 1)

                    def residual(g, n):
                        dve.wait_ge(fin2_mm, n)
                        xs = X[:, bass.ts(g, GB), :]
                        dve.tensor_tensor(xs, PS[:, P_MISC, :].rearrange("s (b d) -> s b d", d=D), xs, ALU.add)\
                           .then_inc(misc2, 1)

                    def ft_lo_step(n):
                        dve.wait_ge(fthi_done, n)
                        dve.tensor_tensor(ft_lo[:], PS[:, P_MISC, :], ft_hi[:].bitcast(F32), ALU.subtract)\
                           .then_inc(misc2, 1)

                    def last_residual(g, n):
                        dve.wait_ge(ff_mm, n)
                        xs = X[:, bass.ts(g, GB), :]
                        dve.tensor_tensor(xs, PS[:, P_MISC, :].rearrange("s (b d) -> s b d", d=D), xs, ALU.add)\
                           .then_inc(misc2, 1)

                    def group(g, first, last):
                        for q in range(NQ):
                            u = NQ * g + q
                            if not (last and q == NQ - 1):
                                if not (first and q == 0):
                                    dve.wait_ge(s_mm, GB * u)
                                g_ev_step((q + 1) % NQ, QH * (u + 1))
                            if q == 2 and not first:
                                residual(g - 1, g)
                            if q == 2 and not last:
                                cy_step(g + 2)
                            if q == 2 and not first:
                                dve.wait_ge(misc2, m_use(g, first, last, 1, "fin") + 1)
                            softmax(q, u)
                            if q == 0 and not last:
                                norm_ctx(g + 1, 2 if first else 3 * g + 1)
                            if q == 1 and not last:
                                norm_lat(g + 1, 3 if first else 3 * g + 2)
                            if q == 2 and not last:
                                ct_lo_step(g + 2)
                            if q == 2 and not first:
                                norm_ffn(g - 1, 3 * g + 1 if last else 3 * g + 3)
                            if q == 3 and not first:
                                ft_lo_step(g)
                            if q == 3 and not first:
                                last_residual(g - 1, g)
                            if q == 3 and not last:
                                lat_step(g + 2)

                    dve.wait_ge(ctx_loaded, 16)
                    norm_ctx(0, 0)
                    norm_lat(0, 1)
                    cy_step(1)
                    ct_lo_step(1)
                    lat_step(1)
                    g_ev_step(0, 0)
                    group(0, True, False)
                    with dve.Fori(1, NG - 1) as g:
                        group(g, False, False)
                    group(NG - 1, False, True)
                    residual(NG - 1, NG)
                    dve.wait_ge(misc2, M_END + 1)
                    norm_ffn(NG - 1, 3 * NG - 1)
                    ft_lo_step(NG)
                    last_residual(NG - 1, NG)


_INS = ['x', 'ctx_1024', 'L0_attn_Wq', 'L0_attn_Wk', 'L0_attn_Wv', 'L0_attn_Wo', 'L0_attn_proj', 'L0_xattn_ln_l_w',
        'L0_xattn_ln_l_b', 'L0_xattn_ln_c_w', 'L0_xattn_ln_c_b', 'L0_xattn_Wq', 'L0_xattn_Wkv', 'L0_xattn_Wo',
        'L0_xattn_bo', 'L0_ffn_weight']


def kernel(**inputs):
    import numpy as _np
    import concourse.bacc as _bacc
    from concourse import mybir as _mybir
    from concourse.bass_utils import run_bass_kernel_spmd as _run

    nc = _bacc.Bacc("TRN2", target_bir_lowering=False, num_devices=1)
    arrays, args = {}, []
    for name in _INS:
        a = _np.ascontiguousarray(inputs[name])
        arrays[f"in_{name}"] = a
        args.append(nc.dram_tensor(f"in_{name}", a.shape, _mybir.dt.from_np(a.dtype), kind="ExternalInput").ap())
    shape = inputs['x'].shape
    args.append(nc.dram_tensor("out_x", shape, _mybir.dt.float32, kind="ExternalOutput").ap())
    decoder_layer(nc, *args)
    r = _run(nc, [arrays], core_ids=[0])
    return r.results[0]["out_x"]
```

```python
import concourse.bass as bass
from concourse import mybir
from contextlib import ExitStack


def decoder_layer(nc, x, ctx_in, wq1, wk1, wv1, wo1, proj, lnl_w, lnl_b, lnc_w, lnc_b,
                  wq2, wkv2, wo2, bo2, w_ffn, out):
    F32 = mybir.dt.float32
    F32R = mybir.dt.float32r
    ALU = mybir.AluOpType
    ACT = mybir.ActivationFunctionType
    AX = mybir.AxisListType

    NB, S, D = x.shape
    C = ctx_in.shape[1]
    HD = proj.shape[0]
    NH = wq1.shape[1] // HD
    NP = NH // 2
    GB = 4
    NG = NB // GB
    W = GB * S
    GC = GB * C
    INNER = NH * HD
    HALF = INNER // 2
    QH = 4
    NQ = NH // QH
    QC = QH * C
    EPS_OUT = 1e-5
    EPS_LN = 1e-5
    EPS_DEN = 1e-6
    SCALE = float(HD) ** -0.5
    EXP_HI, EXP_LO = 59874.141715197817, 1.670170079024566e-05

    stack = ExitStack()
    with stack:
        def sb(name, shape, dt=F32):
            return stack.enter_context(nc.sbuf_tensor(name, shape, dt))

        def sem(name):
            return stack.enter_context(nc.semaphore(name))

        X = sb("X", [128, NB, D])
        CX = sb("CX", [C, NB, D])
        ident = sb("ident", [128, 128])
        causal = sb("causal", [128, 1, S])
        wq1_hi, wq1_lo = sb("wq1_hi", [D, INNER], F32R), sb("wq1_lo", [D, INNER], F32R)
        wk1_hi, wk1_lo = sb("wk1_hi", [D, INNER], F32R), sb("wk1_lo", [D, INNER], F32R)
        wv1_hi, wv1_lo = sb("wv1_hi", [D, INNER], F32R), sb("wv1_lo", [D, INNER], F32R)
        wv2_hi, wv2_lo = sb("wv2_hi", [D, INNER], F32R), sb("wv2_lo", [D, INNER], F32R)
        m_hi, m_lo = sb("m_hi", [D, NH, D], F32R), sb("m_lo", [D, NH, D], F32R)
        wo1_sb = sb("wo1_sb", [128, NP, D])
        wo2_sb = sb("wo2_sb", [128, NP, D])
        sign_t = sb("sign_t", [D, D], F32R)
        lnl_w_sb, lnl_b_sb = sb("lnl_w_sb", [D, 1]), sb("lnl_b_sb", [D, 1])
        lnc_w_sb, lnc_b_sb = sb("lnc_w_sb", [D, 1]), sb("lnc_b_sb", [D, 1])
        bo_sb = sb("bo_sb", [D, 1])

        st6 = sb("st6", [128, GB, 6])
        mean = sb("mean", [128, GB, 1])
        m_sum, m_dif = sb("m_sum", [128, GB]), sb("m_dif", [128, GB])
        sq_sum, sq_dif = sb("sq_sum", [128, GB]), sb("sq_dif", [128, GB])
        var_part = sb("var_part", [128, GB])
        r1 = sb("r1", [128, GB, 1])
        r2 = sb("r2", [128, GB, 1])
        t1 = sb("t1", [128, GB, 1])
        minus_half = sb("minus_half", [128, 16])

        def variance(dve, parts, n, a, b, halves, done):
            p = slice(0, parts)
            dve.tensor_tensor(m_sum[p], st6[p, :, 1], st6[p, :, 4], ALU.add)
            dve.tensor_tensor(m_dif[p], st6[p, :, 1], st6[p, :, 4], ALU.subtract)
            dve.tensor_tensor(sq_sum[p], st6[p, :, 2], st6[p, :, 5], ALU.add).then_inc(halves, 1)
            dve.wait_ge(halves, 2 * n + 1)
            dve.tensor_scalar(mean[p, :, 0], m_sum[p], 0.5, None, ALU.mult)
            dve.tensor_scalar(var_part[p], sq_sum[p], a / D, b, ALU.mult, ALU.add)
            dve.scalar_tensor_tensor(sq_dif[p], m_dif[p], a / 4, m_dif[p], ALU.mult, ALU.mult).then_inc(halves, 1)
            dve.wait_ge(halves, 2 * n + 2)
            dve.tensor_tensor(t1[p, :, 0], var_part[p], sq_dif[p], ALU.add).then_inc(done, 1)

        PS = stack.enter_context(nc.psum_tensor("PS", [128, 8, 512], F32))

        w_loaded = sem("w_loaded")
        wv_loaded = sem("wv_loaded")
        x_in = [sem(f"x_in{i}") for i in range(3)]
        ctx_loaded = sem("ctx_loaded")
        zeroed, consts = sem("zeroed"), sem("consts")
        prep_mm, prep_cp, prep_hi, prep_lo = sem("prep_mm"), sem("prep_cp"), sem("prep_hi"), sem("prep_lo")
        wv_hi_done, wv_done, sign_done = sem("wv_hi_done"), sem("wv_done"), sem("sign_done")
        sign_gt, sign_lt = sem("sign_gt"), sem("sign_lt")
        x_cut = [0, GB, 4 * GB, NB] if NB > 4 * GB else [0, GB, 2 * GB, NB]

        prep_stack = ExitStack()
        with prep_stack:
            def psb(name, shape, dt=F32):
                return prep_stack.enter_context(nc.sbuf_tensor(name, shape, dt))

            raw = [psb(f"raw{i}", [D, INNER]) for i in range(4)]
            rawv = [psb(f"rawv{i}", [D, INNER]) for i in range(2)]
            wt = [psb(f"wt{i}", [128, INNER]) for i in range(4)]
            projbd = psb("projbd", [128, 128])
            ffn_raw, ffn_gt, ffn_lt = psb("ffn_raw", [D, D]), psb("ffn_gt", [D, D]), psb("ffn_lt", [D, D])
            NT = 4 * NP // 4
            NC = 2 * (2 * NP // 8)
            NM = NH // 4
            with nc.Block() as block:

                @block.sync
                def _(sp):
                    for i, src in enumerate([wq1, wk1, wq2]):
                        sp.dma_start(raw[i][:], src).then_inc(w_loaded, 16)
                    sp.dma_start(raw[3][:], wkv2[:, 0:INNER]).then_inc(w_loaded, 16)
                    for c in range(2):
                        sp.dma_start(X[:, x_cut[c]:x_cut[c + 1], :],
                                     x[x_cut[c]:x_cut[c + 1]].rearrange("b s d -> s b d")).then_inc(x_in[c], 16)
                    sp.dma_start(X[:, x_cut[2]:NB, :],
                                 x[x_cut[2]:NB].rearrange("b s d -> s b d")).then_inc(x_in[2], 16)
                    sp.dma_start(CX[:], ctx_in.rearrange("b c d -> c b d")).then_inc(ctx_loaded, 16)

                @block.gpsimd
                def _(pool):
                    pool.memset(projbd[:], 0.0).then_inc(zeroed, 1)
                    pool.memset(ident[:], 0.0).then_inc(zeroed, 1)
                    pool.memset(causal[:], 1.0).then_inc(zeroed, 1)
                    pool.memset(minus_half[:], -0.5).then_inc(zeroed, 1)
                    pool.wait_ge(zeroed, 4)
                    pool.affine_select(out=ident[:], in_=ident[:], compare_op=ALU.not_equal, fill=1.0,
                                       base=0, pattern=[[-1, 128]], channel_multiplier=1).then_inc(consts, 1)
                    pool.affine_select(out=causal[:, 0, :], in_=causal[:, 0, :], compare_op=ALU.is_ge, fill=0.0,
                                       base=0, pattern=[[1, S]], channel_multiplier=-1).then_inc(consts, 1)

                @block.tensor
                def _(pe):
                    pe.wait_ge(consts, 2)
                    pe.wait_ge(w_loaded, 13 * 16)
                    bank = [0]

                    def next_bank():
                        if bank[0] >= 2:
                            pe.wait_ge(prep_cp, bank[0] - 1)
                        b = PS[:, bank[0] % 2, :]
                        bank[0] += 1
                        return b

                    for i in range(4):
                        for c in range(0, NP, 4):
                            b = next_bank()
                            for k in range(4):
                                at = (c + k) * 128
                                mm = pe.transpose(b[:, k * 128:(k + 1) * 128], raw[i][:, at:at + 128], ident[:])
                            mm.then_inc(prep_mm, 1)
                    pe.wait_ge(prep_cp, NT)
                    for i in range(2):
                        for c in range(0, NP, 4):
                            b = next_bank()
                            for k in range(4):
                                at = (c + k) * 128
                                mm = pe.matmul(b[:, k * 128:(k + 1) * 128], wt[i][:, at:at + 128], projbd[:],
                                               start=True, stop=True)
                            mm.then_inc(prep_mm, 1)
                    for c in range(0, NH, 4):
                        b = next_bank()
                        for k in range(4):
                            h = (c // 8) * 8 + (c // 4) % 2 + 2 * k
                            r, at = HD * (h % 2), (h // 2) * 128
                            mm = pe.matmul(b[:, k * 128:(k + 1) * 128], wt[3][r:r + HD, at:at + 128],
                                           wt[2][r:r + HD, at:at + 128], start=True, stop=True)
                        mm.then_inc(prep_mm, 1)
                    b = next_bank()
                    pe.transpose(b[:, 0:128], ffn_raw[:], ident[:]).then_inc(prep_mm, 1)

                dests = []
                for hi, lo in ((wq1_hi, wq1_lo), (wk1_hi, wk1_lo)):
                    for c in range(0, NP, 4):
                        dests.append((hi[:, c * 128:(c + 4) * 128], lo[:, c * 128:(c + 4) * 128]))
                for c in range(0, NH, 4):
                    h = (c // 8) * 8 + (c // 4) % 2
                    dests.append((m_hi[:, h:h + 7:2, :], m_lo[:, h:h + 7:2, :]))

                @block.scalar
                def _(act):
                    act.wait_ge(zeroed, 3)
                    act.dma_start(projbd[0:HD, 0:HD], proj).then_inc(w_loaded, 16)
                    act.dma_start(projbd[HD:128, HD:128], proj).then_inc(w_loaded, 16)
                    act.dma_start(ffn_raw[:], w_ffn).then_inc(w_loaded, 16)
                    for dst, src in ((lnl_w_sb, lnl_w), (lnl_b_sb, lnl_b), (lnc_w_sb, lnc_w), (lnc_b_sb, lnc_b),
                                     (bo_sb, bo2)):
                        act.dma_start(dst[:], src.rearrange("(d o) -> d o", o=1)).then_inc(w_loaded, 16)
                    act.dma_start(wo1_sb[:], wo1.rearrange("(p r) d -> r p d", r=128)).then_inc(w_loaded, 16)
                    act.dma_start(rawv[0][:], wv1).then_inc(wv_loaded, 16)
                    act.dma_start(rawv[1][:], wkv2[:, INNER:2 * INNER]).then_inc(wv_loaded, 16)
                    act.dma_start(wo2_sb[:], wo2.rearrange("(p r) d -> r p d", r=128)).then_inc(wv_loaded, 16)
                    for n in range(NT):
                        act.wait_ge(prep_mm, n + 1)
                        i, c = n // (NP // 4), n % (NP // 4)
                        act.activation(wt[i][:, c * 512:(c + 1) * 512], PS[:, n % 2, :], ACT.Copy).then_inc(prep_cp, 1)
                    for n, (hi, _) in enumerate(dests):
                        act.wait_ge(prep_mm, NT + n + 1)
                        act.activation(hi, PS[:, (NT + n) % 2, :], ACT.Copy).then_inc(prep_hi, 1)
                    act.wait_ge(wv_loaded, 48)
                    for i, hi in enumerate((wv1_hi, wv2_hi)):
                        act.activation(hi[:], rawv[i][:], ACT.Copy).then_inc(wv_hi_done, 1)

                @block.vector
                def _(dve):
                    for n, (hi, lo) in enumerate(dests):
                        dve.wait_ge(prep_hi, n + 1)
                        dve.tensor_tensor(lo, PS[:, (NT + n) % 2, :], hi.bitcast(F32), ALU.subtract).then_inc(prep_cp, 1)
                    dve.wait_ge(wv_loaded, 48)
                    for i, (hi, lo) in enumerate(((wv1_hi, wv1_lo), (wv2_hi, wv2_lo))):
                        dve.wait_ge(wv_hi_done, i + 1)
                        dve.tensor_tensor(lo[:], rawv[i][:], hi[:].bitcast(F32), ALU.subtract).then_inc(wv_done, 1)
                    last = NT + len(dests)
                    dve.wait_ge(prep_mm, last + 1)
                    dve.tensor_scalar(ffn_gt[:], PS[:, last % 2, 0:D], 0.0, None, ALU.is_gt).then_inc(sign_gt, 1)
                    dve.tensor_scalar(ffn_lt[:], PS[:, last % 2, 0:D], 0.0, None, ALU.is_lt).then_inc(sign_lt, 1)
                    dve.wait_ge(sign_gt, 1)
                    dve.wait_ge(sign_lt, 1)
                    dve.tensor_tensor(sign_t[:], ffn_gt[:], ffn_lt[:], ALU.subtract).then_inc(sign_done, 1)

        with ExitStack() as pa:
            def asb(name, shape, dt=F32):
                return pa.enter_context(nc.sbuf_tensor(name, shape, dt))

            def asem(name):
                return pa.enter_context(nc.semaphore(name))

            xn = asb("a_xn", [128, GB, D])
            xt_hi, xt_lo = asb("a_xt_hi", [D, W], F32R), asb("a_xt_lo", [D, W], F32R)
            xtn_hi, xtn_lo = asb("a_xtn_hi", [D, W], F32R), asb("a_xtn_lo", [D, W], F32R)
            e_q, e_k = asb("a_e_q", [128, W]), asb("a_e_k", [128, W])
            fq = asb("a_fq", [128, 2, W])
            fk = asb("a_fk", [128, 2, W])
            am = asb("a_am", [128, 2, 2, GB, S])
            v = asb("a_v", [128, GB, NH, HD + 1])
            den = asb("a_den", [128, 2, GB, 1])
            rden = asb("a_rden", [128, 2, GB, 1])
            on = asb("a_on", [128, 2, GB, 2, HD])
            ot = asb("a_ot", [128, 2, W])
            acc_sb = asb("a_acc_sb", [D, W])

            B_QK, B_MISC, B_A, B_O, B_OT, B_ACC = 0, 1, 2, 4, 6, 7

            q_proj, k_proj = asem("q_proj"), asem("k_proj")
            nq_done, nk_done = asem("nq_done"), asem("nk_done")
            eq_done, ek_done = asem("eq_done"), asem("ek_done")
            fq_done, fk_done = asem("fq_done"), asem("fk_done")
            a_done, mask_done = asem("a_done"), asem("mask_done")
            av_done, norm_done = asem("av_done"), asem("norm_done")
            den_done, rden_done = asem("den_done"), asem("rden_done")
            ot_done, ote_done, wo_done = asem("ot_done"), asem("ote_done"), asem("wo_done")
            v_mm = asem("v_mm")
            misc_free = asem("misc_free")
            acc_evac, fin_done = asem("acc_evac"), asem("fin_done")
            ln_st, ln_mv, ln_v = asem("ln_st"), asem("ln_mv"), asem("ln_v")
            ln_r, xn_ready = asem("ln_r"), asem("xn_ready")
            xt_done, xthi_done, cur_ready = asem("xt_done"), asem("xthi_done"), asem("cur_ready")
            ones_set = asem("ones_set")

            N_PRO = 1 + GB

            def use(g, first, p, kind):
                i = p + (1 if p > 3 else 0)
                if kind == "xt":
                    i = 4
                if not first and (p > 1 or kind == "fin"):
                    i += 1
                return (N_PRO if first else 10 * g + 4) + (i if not (kind == "fin") else 2)

            def ln_factor(dve, g, n):
                for b in range(GB):
                    i = dve.bn_stats(st6[:, b, :], X[:, g * GB + b, :])
                i.then_inc(ln_st, 1)
                dve.wait_ge(ln_st, n + 1)
                variance(dve, 128, n, 1.0, EPS_OUT, ln_mv, ln_v)

            def ln_apply(dve, g, n):
                dve.wait_ge(ln_r, n + 1)
                for b in range(GB):
                    i = dve.tensor_scalar(xn[:, b, :], X[:, g * GB + b, :], mean[:, b, :], r1[:, b, :],
                                          ALU.subtract, ALU.mult)
                i.then_inc(xn_ready, 1)

            def split3(pe, dst, w_hi, w_lo, x_hi, x_lo):
                pe.matmul(dst, w_hi, x_hi, start=True, stop=False)
                pe.matmul(dst, w_hi, x_lo, start=False, stop=False)
                return pe.matmul(dst, w_lo, x_hi, start=False, stop=True)

            def v_args(b, half, hi, lo):
                s, c = slice(b * S, (b + 1) * S), slice(half * HALF, (half + 1) * HALF)
                return hi[:, s], lo[:, s], wv1_hi[:, c], wv1_lo[:, c]

            with nc.Block() as block:

                @block.sync
                def _(sp):
                    sp.wait_ge(x_in[2], 16)

                @block.tensor
                def _(pe):
                    def xt_transposes(g, i):
                        pe.wait_ge(xn_ready, g + 1)
                        if not (isinstance(i, int) and i == 0):
                            pe.wait_ge(misc_free, i)
                        for b in range(GB):
                            mm = pe.transpose(PS[:, B_MISC, b * S:(b + 1) * S], xn[:, b, :], ident[:])
                        mm.then_inc(xt_done, 1)

                    def v_half(b, half, hi, lo, i):
                        pe.wait_ge(misc_free, i)
                        split3(pe, PS[:, B_MISC, :], *v_args(b, half, hi, lo)).then_inc(v_mm, 1)

                    def proj_step(p, w_hi, w_lo, hi, lo, done):
                        c = slice(p * 128, (p + 1) * 128)
                        split3(pe, PS[:, B_QK, :], w_hi[:, c], w_lo[:, c], hi[:], lo[:]).then_inc(done, 1)

                    def transposes_and_v0():
                        pe.wait_ge(wv_done, 2)
                        xt_transposes(0, 0)
                        for b in range(GB):
                            v_half(b, 0, xtn_hi, xtn_lo, 1 + b)

                    def wo_step(p):
                        mm = pe.matmul(PS[:, B_ACC, :], wo1_sb[:, p, :], ot[:, p % 2, :],
                                       start=(p == 0), stop=(p == NP - 1))
                        mm.then_inc(wo_done, 1)

                    def fin_transposes(i, n):
                        pe.wait_ge(acc_evac, n)
                        pe.wait_ge(misc_free, i)
                        for b in range(GB):
                            mm = pe.transpose(PS[:, B_MISC, b * S:(b + 1) * S], acc_sb[:, b * S:(b + 1) * S], ident[:])
                        mm.then_inc(fin_done, 1)

                    def ot_transposes(p):
                        for b in range(GB):
                            mm = pe.transpose(PS[:, B_OT, b * S:(b + 1) * S],
                                              on[:, p % 2, b, :, :].rearrange("s h d -> s (h d)"), ident[:])
                        mm.then_inc(ot_done, 1)

                    def group(g, first, last):
                        for p in range(NP):
                            u = NP * g + p
                            begin = first and p == 0
                            more = not (last and p == NP - 1)
                            nxt = (p + 1) % NP
                            hi, lo = (xtn_hi, xtn_lo) if p == NP - 1 else (xt_hi, xt_lo)
                            if more:
                                if p == 0:
                                    pe.wait_ge(cur_ready, g + 1)
                                if p == NP - 1:
                                    pe.wait_ge(misc_free, use(g, first, 3, "xt") + 1)
                                pe.wait_ge(fk_done, u + 1)
                                proj_step(nxt, wq1_hi, wq1_lo, hi, lo, q_proj)
                            pe.wait_ge(fq_done, u + 1)
                            pe.wait_ge(fk_done, u + 1)
                            if not begin:
                                pe.wait_ge(mask_done, 2 * u)
                            for b in range(GB):
                                for h in range(2):
                                    r = slice(h * HD, (h + 1) * HD)
                                    c = slice(b * S, (b + 1) * S)
                                    mm = pe.matmul(PS[:, B_A + h, c], fk[r, p % 2, c], fq[r, p % 2, c],
                                                   start=True, stop=True)
                            mm.then_inc(a_done, 1)
                            if p < GB:
                                v_half(p, 1, xt_hi, xt_lo, use(g, first, p, "v"))
                            elif not last:
                                v_half(p - GB, 0, xtn_hi, xtn_lo, use(g, first, p, "v"))
                            if not begin:
                                pe.wait_ge(norm_done, u)
                                if not (first and p == 1):
                                    pe.wait_ge(ote_done, u - 1)
                                ot_transposes((p - 1) % NP)
                            if more:
                                pe.wait_ge(fq_done, u + 2)
                                proj_step(nxt, wk1_hi, wk1_lo, hi, lo, k_proj)
                            if p == 0:
                                pe.wait_ge(misc_free, use(g, first, 0, "v"))
                            if p == GB:
                                pe.wait_ge(misc_free, use(g, first, 3, "v") + 1)
                            for h in range(2):
                                pe.wait_ge(mask_done, 2 * u + 1 + h)
                                for b in range(GB):
                                    mm = pe.matmul(PS[:, B_O + h, b * (HD + 1):(b + 1) * (HD + 1)],
                                                   am[:, p % 2, h, b, :], v[:, b, 2 * p + h, :], start=True, stop=True)
                            mm.then_inc(av_done, 1)
                            if not begin:
                                pe.wait_ge(ote_done, u)
                                if p == 1 and not first:
                                    pe.wait_ge(acc_evac, g)
                                wo_step((p - 1) % NP)
                            if p == 1 and not first:
                                fin_transposes(use(g, first, 1, "fin"), g)
                            if p == 3 and not last:
                                xt_transposes(g + 1, use(g, first, 3, "xt"))

                    transposes_and_v0()
                    proj_step(0, wq1_hi, wq1_lo, xtn_hi, xtn_lo, q_proj)
                    pe.wait_ge(fq_done, 1)
                    proj_step(0, wk1_hi, wk1_lo, xtn_hi, xtn_lo, k_proj)
                    group(0, True, False)
                    with pe.Fori(1, NG - 1) as g:
                        group(g, False, False)
                    group(NG - 1, False, True)
                    U = NP * NG
                    pe.wait_ge(norm_done, U)
                    pe.wait_ge(ote_done, U - 1)
                    ot_transposes(NP - 1)
                    pe.wait_ge(ote_done, U)
                    wo_step(NP - 1)
                    fin_transposes(use(NG - 1, False, 3, "v") + 1, NG)

                @block.scalar
                def _(act):
                    def exp_step(u1, mm, e, read, negative, done):
                        act.wait_ge(mm, u1)
                        if read is not None:
                            act.wait_ge(*read)
                        act.activation(e[:], PS[:, B_QK, :], ACT.Relu, scale=-1.0).then_inc(negative, 1)
                        act.wait_ge(negative, u1)
                        act.activation(e[:], e[:], ACT.Exp, scale=-1.0).then_inc(done, 1)

                    def v_evac(b, half, n):
                        act.wait_ge(v_mm, n)
                        act.activation(v[:, b, half * NP:(half + 1) * NP, 0:HD],
                                       PS[:, B_MISC, :].rearrange("s (h d) -> s h d", d=HD),
                                       ACT.Copy).then_inc(misc_free, 1)

                    def ot_evac(p, n):
                        act.wait_ge(ot_done, n)
                        act.activation(ot[:, p % 2, :], PS[:, B_OT, :], ACT.Copy).then_inc(ote_done, 1)

                    def xt_hi_evac(n):
                        act.wait_ge(xt_done, n)
                        act.activation(xtn_hi[:], PS[:, B_MISC, :], ACT.Copy).then_inc(xthi_done, 1)

                    def copy_over():
                        act.activation(xt_hi[:], xtn_hi[:].bitcast(F32), ACT.Copy)
                        act.activation(xt_lo[:], xtn_lo[:].bitcast(F32), ACT.Copy).then_inc(cur_ready, 1)

                    def acc_to_sbuf(n):
                        act.wait_ge(wo_done, NP * n)
                        act.activation(acc_sb[:], PS[:, B_ACC, :], ACT.Copy).then_inc(acc_evac, 1)

                    def group(g, first, last):
                        for p in range(NP):
                            u = NP * g + p
                            begin = first and p == 0
                            more = not (last and p == NP - 1)
                            if p == 1 and not first:
                                acc_to_sbuf(g)
                            if more:
                                exp_step(u + 2, q_proj, e_q, (fq_done, u + 1), nq_done, eq_done)
                            if p < GB:
                                if not first:
                                    act.wait_ge(av_done, NP * g)
                                v_evac(p, 1, u + GB + 1)
                            elif not last:
                                act.wait_ge(av_done, u - p + NP // 2)
                                v_evac(p - GB, 0, u + GB + 1)
                            if not begin:
                                if not (first and p < 3):
                                    act.wait_ge(wo_done, u - 2)
                                ot_evac((p - 1) % NP, u)
                            if more:
                                exp_step(u + 2, k_proj, e_k, (fk_done, u + 1), nk_done, ek_done)
                            if p == 3 and not last:
                                xt_hi_evac(g + 2)
                            if p == NP - 1 and not last:
                                act.wait_ge(k_proj, u + 1)
                                act.wait_ge(misc_free, use(g, first, 3, "xt") + 1)
                                copy_over()

                    xt_hi_evac(1)
                    act.wait_ge(misc_free, 1)
                    copy_over()
                    for b in range(GB):
                        v_evac(b, 0, b + 1)
                    exp_step(1, q_proj, e_q, None, nq_done, eq_done)
                    exp_step(1, k_proj, e_k, None, nk_done, ek_done)
                    group(0, True, False)
                    with act.Fori(1, NG - 1) as g:
                        group(g, False, False)
                    group(NG - 1, False, True)
                    act.wait_ge(wo_done, NP * NG - 2)
                    ot_evac(NP - 1, NP * NG)
                    acc_to_sbuf(NG)

                @block.gpsimd
                def _(pool):
                    def factor(n):
                        pool.wait_ge(ln_v, n + 1)
                        pool.tensor_tensor(r1[:, :, 0], t1[:, :, 0], minus_half[:, 0:GB], ALU.pow).then_inc(ln_r, 1)

                    pool.memset(v[:, :, :, HD:HD + 1], 1.0).then_inc(ones_set, 1)
                    pool.wait_ge(zeroed, 4)
                    factor(0)
                    with pool.Fori(1, NG) as g:
                        factor(g)

                @block.vector
                def _(dve):
                    def feature(u1, par, e, ready, f, done):
                        dve.wait_ge(ready, u1)
                        dve.scalar_tensor_tensor(f[:, par, :], PS[:, B_QK, :], 0.0, e[:], ALU.max, ALU.add)\
                           .then_inc(done, 1)

                    def mask(p, h, n):
                        dve.wait_ge(a_done, n)
                        dve.tensor_tensor(am[:, p % 2, h], PS[:, B_A + h, :].rearrange("k (b s) -> k b s", s=S),
                                          causal[:].broadcast_to([128, GB, S]), ALU.mult).then_inc(mask_done, 1)

                    def normalise(p, n, wait_ot):
                        dve.wait_ge(av_done, n)
                        o = PS[:, B_O:B_O + 2, 0:GB * (HD + 1)].rearrange("s h (b e) -> s h b e", e=HD + 1)
                        dve.tensor_scalar(den[:, :, :, 0], o[:, :, :, HD], EPS_DEN, None, ALU.add).then_inc(den_done, 1)
                        dve.wait_ge(den_done, n)
                        dve.reciprocal(rden[:], den[:]).then_inc(rden_done, 1)
                        dve.wait_ge(rden_done, n)
                        if wait_ot is not None:
                            dve.wait_ge(ot_done, wait_ot)
                        dve.tensor_tensor(on[:, p % 2].rearrange("s b h d -> s h b d"), o[:, :, :, 0:HD],
                                          rden[:].broadcast_to([128, 2, GB, HD]), ALU.mult).then_inc(norm_done, 1)

                    def xt_lo_evac(n):
                        dve.wait_ge(xthi_done, n)
                        dve.tensor_tensor(xtn_lo[:], PS[:, B_MISC, :], xtn_hi[:].bitcast(F32), ALU.subtract)\
                           .then_inc(misc_free, 1)

                    def residual(g, n):
                        dve.wait_ge(fin_done, n)
                        xs = X[:, bass.ts(g, GB), :]
                        dve.tensor_tensor(xs, PS[:, B_MISC, :].rearrange("s (b d) -> s b d", d=D), xs, ALU.add)\
                           .then_inc(misc_free, 1)

                    def group(g, first, last):
                        for p in range(NP):
                            u = NP * g + p
                            begin = first and p == 0
                            more = not (last and p == NP - 1)
                            if not (first and p < 2):
                                dve.wait_ge(av_done, u - 1)
                            if p == 4 and not last:
                                xt_lo_evac(g + 2)
                            if p == 2 and not first:
                                residual(g - 1, g)
                            if more:
                                feature(u + 2, (p + 1) % 2, e_q, eq_done, fq, fq_done)
                            mask(p, 0, u + 1)
                            mask(p, 1, u + 1)
                            if p == 0 and not last:
                                if first:
                                    dve.wait_ge(x_in[1], 16)
                                ln_factor(dve, g + 1, g + 1)
                            if p == 1 and not last:
                                ln_apply(dve, g + 1, g + 1)
                            if more:
                                feature(u + 2, (p + 1) % 2, e_k, ek_done, fk, fk_done)
                            normalise(p, u + 1, None if first and p < 2 else u - 1)

                    dve.wait_ge(x_in[0], 16)
                    ln_factor(dve, 0, 0)
                    ln_apply(dve, 0, 0)
                    xt_lo_evac(1)
                    dve.wait_ge(ones_set, 1)
                    feature(1, 0, e_q, eq_done, fq, fq_done)
                    feature(1, 0, e_k, ek_done, fk, fk_done)
                    group(0, True, False)
                    dve.wait_ge(x_in[2], 16)
                    with dve.Fori(1, NG - 1) as g:
                        group(g, False, False)
                    group(NG - 1, False, True)
                    residual(NG - 1, NG)

        with ExitStack() as pb:
            def bsb(name, shape, dt=F32):
                return pb.enter_context(nc.sbuf_tensor(name, shape, dt))

            def bsem(name):
                return pb.enter_context(nc.semaphore(name))

            cn = bsb("b_cn", [C, GB, D])
            cy = bsb("b_cy", [D, GC])
            ct_hi, ct_lo = bsb("b_ct_hi", [D, GC], F32R), bsb("b_ct_lo", [D, GC], F32R)
            ctn_hi, ctn_lo = bsb("b_ctn_hi", [D, GC], F32R), bsb("b_ctn_lo", [D, GC], F32R)
            ln_x = bsb("b_ln_x", [128, GB, D])
            lat_t = bsb("b_lat_t", [D, W])
            gs = bsb("b_gs", [D, 2, GB, QC])
            e = bsb("b_e", [128, 2, GB, QC])
            sums = bsb("b_sums", [128, GB * QH])
            rsum = bsb("b_rsum", [128, GB * QH, 1])
            pt = bsb("b_pt", [C, GB, QH, S])
            v2 = bsb("b_v2", [C, GB, NH, HD])
            ot2 = bsb("b_ot2", [128, 2, W])
            acc2_sb = bsb("b_acc_sb", [D, W])
            fn = bsb("b_fn", [128, GB, D])
            ft_hi, ft_lo = bsb("b_ft_hi", [D, W], F32R), bsb("b_ft_lo", [D, W], F32R)

            P_ACC, P_G, P_S, P_PT, P_MISC = 0, 1, 3, 5, 7

            g_mm, g_ev = bsem("g_mm"), bsem("g_ev")
            s_mm, s_ev = bsem("s_mm"), bsem("s_ev")
            clipped, summed, inverted, p_ready = bsem("clipped"), bsem("summed"), bsem("inverted"), bsem("p_ready")
            pt_mm, pt_ev = bsem("pt_mm"), bsem("pt_ev")
            pv_mm, ot_ev, wo_mm = bsem("pv_mm"), bsem("ot_ev"), bsem("wo_mm")
            v2_mm = bsem("v2_mm")
            misc2 = bsem("misc2")
            acc2_ev, fin2_mm = bsem("acc2_ev"), bsem("fin2_mm")
            st_done, mv_done, var_done, f_done = bsem("st_done"), bsem("mv_done"), bsem("var_done"), bsem("f_done")
            cn_ready, lnx_ready, fn_ready = bsem("cn_ready"), bsem("lnx_ready"), bsem("fn_ready")
            ct_mm, cthi_done, ctn_ready, ct_cur = bsem("ct_mm"), bsem("cthi_done"), bsem("ctn_ready"), bsem("ct_cur")
            lt_mm = bsem("lt_mm")
            ft_mm, fthi_done, ff_mm = bsem("ft_mm"), bsem("fthi_done"), bsem("ff_mm")
            x_out = bsem("x_out")

            M_PRO = 3

            def m_use(g, first, last, q, kind, i=0):
                order = []
                for qq in range(NQ):
                    if qq == 0:
                        order.append((qq, "lt", 0))
                    if qq == 2 and not last:
                        order.append((qq, "ct", 0))
                    if qq == 3 and not first:
                        order += [(qq, "ft", 0), (qq, "ff", 0)]
                    if not (last and qq == 3):
                        order += [(qq, "v", 0), (qq, "v", 1)]
                    if qq == 1 and not first:
                        order.append((qq, "fin", 0))
                return (M_PRO if first else 13 * g) + order.index((q, kind, i))

            M_END = 13 * (NG - 1) + 10

            def norm_factor(dve, src, parts, n, a, b):
                for k in range(GB):
                    i = dve.bn_stats(st6[0:parts, k, :], src(k))
                i.then_inc(st_done, 1)
                dve.wait_ge(st_done, n + 1)
                variance(dve, parts, n, a, b, mv_done, var_done)

            def norm_apply(dve, src, dst, parts, n, ready):
                dve.wait_ge(f_done, n + 1)
                for k in range(GB):
                    i = dve.tensor_scalar(dst[0:parts, k, :], src(k), mean[0:parts, k, :], r1[0:parts, k, :],
                                          ALU.subtract, ALU.mult)
                i.then_inc(ready, 1)

            with nc.Block() as block:

                @block.sync
                def _(sp):
                    def store(g, i):
                        sp.wait_ge(misc2, i + 1)
                        sp.dma_start(out[bass.ts(g, GB)].rearrange("b s d -> s b d"), X[:, bass.ts(g, GB), :])\
                          .then_inc(x_out, 16)

                    with sp.Fori(0, NG - 2) as g:
                        store(g, 13 * g + 23)
                    store(NG - 2, M_END - 1)
                    store(NG - 1, M_END + 2)
                    sp.wait_ge(x_out, 16 * NG)

                @block.gpsimd
                def _(pool):
                    with pool.Fori(0, 3 * NG) as n:
                        pool.wait_ge(var_done, n + 1)
                        pool.tensor_tensor(r1[:, :, 0], t1[:, :, 0], minus_half[:, 0:GB], ALU.pow).then_inc(f_done, 1)

                @block.tensor
                def _(pe):
                    def three(dst, w_hi, w_lo, x_hi, x_lo):
                        pe.matmul(dst, w_hi, x_hi, start=True, stop=False)
                        pe.matmul(dst, w_hi, x_lo, start=False, stop=False)
                        return pe.matmul(dst, w_lo, x_hi, start=False, stop=True)

                    def g_heads(q, heads, hi, lo, base):
                        for i in heads:
                            h = QH * q + i
                            if not (isinstance(base, int) and base + i < 2):
                                pe.wait_ge(g_ev, base + i - 1)
                            three(PS[:, P_G + i % 2, 0:GC], m_hi[:, h, :], m_lo[:, h, :], hi[:], lo[:]).then_inc(g_mm, 1)

                    def v_step(b, half, hi, lo, i):
                        pe.wait_ge(misc2, i)
                        s, c = slice(b * C, (b + 1) * C), slice(half * HALF, (half + 1) * HALF)
                        three(PS[0:C, P_MISC, :], hi[:, s], lo[:, s], wv2_hi[:, c], wv2_lo[:, c]).then_inc(v2_mm, 1)

                    def four_transposes(src, done):
                        for b in range(GB):
                            mm = pe.transpose(PS[:, P_MISC, b * S:(b + 1) * S], src(b), ident[:])
                        mm.then_inc(done, 1)

                    def ct_transposes(n, i):
                        pe.wait_ge(cn_ready, n)
                        if i is not None:
                            pe.wait_ge(misc2, i)
                        for b in range(GB):
                            mm = pe.transpose(PS[:, P_MISC, b * C:(b + 1) * C], cn[:, b, :], ident[0:C, 0:C])
                        mm.then_inc(ct_mm, 1)

                    def lt_transposes(n, i):
                        pe.wait_ge(lnx_ready, n)
                        pe.wait_ge(misc2, i)
                        four_transposes(lambda b: ln_x[:, b, :], lt_mm)

                    def fin_transposes(n, i):
                        pe.wait_ge(acc2_ev, n)
                        pe.wait_ge(misc2, i)
                        four_transposes(lambda b: acc2_sb[:, b * S:(b + 1) * S], fin2_mm)

                    def ft_transposes(n, i):
                        pe.wait_ge(fn_ready, n)
                        pe.wait_ge(misc2, i)
                        four_transposes(lambda b: fn[:, b, :], ft_mm)

                    def ffn(i_ft, i):
                        pe.wait_ge(misc2, i_ft + 1)
                        pe.wait_ge(misc2, i)
                        for b in range(GB):
                            s = slice(b * S, (b + 1) * S)
                            pe.matmul(PS[:, P_MISC, s], ft_hi[:, s], sign_t[:], start=True, stop=False)
                            mm = pe.matmul(PS[:, P_MISC, s], ft_lo[:, s], sign_t[:], start=False, stop=True)
                        mm.then_inc(ff_mm, 1)

                    def wo_step(q, n):
                        for pp in range(2):
                            pe.wait_ge(ot_ev, 2 * (n - 1) + pp + 1)
                            k = 2 * q + pp
                            mm = pe.matmul(PS[:, P_ACC, :], wo2_sb[:, k, :], ot2[:, pp, :],
                                           start=(k == 0), stop=(k == NP - 1))
                        mm.then_inc(wo_mm, 1)

                    def scores(q, u, bs, begin):
                        pe.wait_ge(g_ev, QH * (u + 1))
                        for b in bs:
                            if b < 2 and not begin:
                                pe.wait_ge(ot_ev, 2 * (u - 2) + b + 1)
                            elif b >= 2 or not (isinstance(u, int) and u == 0):
                                pe.wait_ge(s_ev, GB * u + b - 1)
                            pe.matmul(PS[:, P_S + b % 2, 0:QC], lat_t[:, b * S:(b + 1) * S], gs[:, q % 2, b, :],
                                      start=True, stop=True).then_inc(s_mm, 1)

                    def pt_part(q, v, bs, begin):
                        pe.wait_ge(p_ready, v + 1)
                        for b in bs:
                            if not (begin and b < 2):
                                pe.wait_ge(pt_ev, GB * v + b - 1)
                            for i in range(QH):
                                mm = pe.transpose(PS[0:C, P_PT + b % 2, i * S:(i + 1) * S],
                                                  e[:, q % 2, b, i * C:(i + 1) * C], ident[:])
                            mm.then_inc(pt_mm, 1)

                    def pv_part(q, v, bs):
                        pe.wait_ge(pt_ev, GB * v + bs[-1] + 1)
                        for pp in range(2):
                            for b in bs:
                                for i in range(2):
                                    mm = pe.matmul(PS[i * HD:(i + 1) * HD, P_S + pp, b * S:(b + 1) * S],
                                                   v2[:, b, QH * q + 2 * pp + i, :], pt[:, b, 2 * pp + i, :],
                                                   start=True, stop=True)
                            if bs[-1] == GB - 1:
                                mm.then_inc(pv_mm, 1)

                    def group(g, first, last):
                        for q in range(NQ):
                            u = NQ * g + q
                            more = not (last and q == NQ - 1)

                            def at(kind, i=0):
                                return m_use(g, first, last, q, kind, i)
                            hi, lo = (ctn_hi, ctn_lo) if q == NQ - 1 else (ct_hi, ct_lo)
                            if more:
                                if q == 0:
                                    pe.wait_ge(ct_cur, g + 1)
                                if q == NQ - 1:
                                    pe.wait_ge(ctn_ready, g + 2)
                                g_heads((q + 1) % NQ, (0, 1), hi, lo, QH * (u + 1))
                            if q == 0:
                                lt_transposes(g + 1, at("lt"))
                            if not (first and q < 2):
                                if q == 2 and not first:
                                    pe.wait_ge(acc2_ev, g)
                                wo_step((q - 2) % NQ, u - 1)
                            if q == 0:
                                pe.wait_ge(misc2, at("lt") + 1)
                            scores(q, u, (0, 1), first and q < 2)
                            if more:
                                g_heads((q + 1) % NQ, (2, 3), hi, lo, QH * (u + 1))
                            scores(q, u, (2, 3), first and q < 2)
                            if q == 2 and not last:
                                ct_transposes(g + 2, at("ct"))
                            if q == 3 and not first:
                                ft_transposes(g, at("ft"))

                            def v_turn(i):
                                if q == 0:
                                    v_step(2 + i, 0, ct_hi, ct_lo, at("v", i))
                                elif q < 3:
                                    v_step(2 * q - 2 + i, 1, ct_hi, ct_lo, at("v", i))
                                elif not last:
                                    v_step(i, 0, ctn_hi, ctn_lo, at("v", i))

                            previous = not (first and q == 0)
                            if previous:
                                pt_part((q - 1) % NQ, u - 1, (0, 1), first and q == 1)
                            if q < 3:
                                v_turn(0)
                            if previous:
                                pt_part((q - 1) % NQ, u - 1, (2, 3), first and q == 1)
                            if q == 3 and not first:
                                ffn(at("ft"), at("ff"))
                            if previous:
                                if q == 1:
                                    pe.wait_ge(misc2, m_use(g, first, last, 0, "v", 1) + 1)
                                if q == 3:
                                    pe.wait_ge(misc2, m_use(g, first, last, 2, "v", 1) + 1)
                                pe.wait_ge(s_ev, GB * (u + 1))
                                pv_part((q - 1) % NQ, u - 1, (0, 1))
                            v_turn(1 if q < 3 else 0)
                            if previous:
                                pv_part((q - 1) % NQ, u - 1, (2, 3))
                            if q == 3:
                                v_turn(1)
                            if q == 1 and not first:
                                fin_transposes(g, at("fin"))

                    pe.wait_ge(consts, 2)
                    ct_transposes(1, None)
                    pe.wait_ge(ctn_ready, 1)
                    v_step(0, 0, ctn_hi, ctn_lo, 1)
                    g_heads(0, range(QH), ctn_hi, ctn_lo, 0)
                    v_step(1, 0, ctn_hi, ctn_lo, 2)
                    group(0, True, False)
                    with pe.Fori(1, NG - 1) as g:
                        group(g, False, False)
                    group(NG - 1, False, True)
                    U = NQ * NG
                    wo_step(NQ - 2, U - 1)
                    pt_part(NQ - 1, U - 1, range(GB), False)
                    pv_part(NQ - 1, U - 1, range(GB))
                    wo_step(NQ - 1, U)
                    fin_transposes(NG, M_END)
                    ft_transposes(NG, M_END + 1)
                    ffn(M_END + 1, M_END + 2)

                @block.scalar
                def _(act):
                    def copy(dst, src, done):
                        act.activation(dst, src, ACT.Copy).then_inc(done, 1)

                    def ct_hi_step(i):
                        act.wait_ge(misc2, i + 1)
                        copy(ctn_hi[:], cy[:], cthi_done)

                    def copy_over():
                        act.activation(ct_hi[:], ctn_hi[:].bitcast(F32), ACT.Copy)
                        copy(ct_lo[:], ctn_lo[:].bitcast(F32), ct_cur)

                    def v_ev(b, half, n):
                        act.wait_ge(v2_mm, n)
                        copy(v2[:, b, half * NP:(half + 1) * NP, :],
                             PS[0:C, P_MISC, :].rearrange("c (h d) -> c h d", d=HD), misc2)

                    def exp_part(q, u, bs):
                        for b in bs:
                            act.wait_ge(s_mm, GB * u + b + 1)
                            act.activation(e[:, q % 2, b, :], PS[:, P_S + b % 2, 0:QC], ACT.Exp, scale=SCALE)\
                               .then_inc(s_ev, 1)

                    def g_ev_part(q, base, heads):
                        for i in heads:
                            act.wait_ge(g_mm, base + i + 1)
                            copy(gs[:, q % 2, :, i * C:(i + 1) * C],
                                 PS[:, P_G + i % 2, 0:GC].rearrange("p (b c) -> p b c", c=C), g_ev)

                    def pt_ev_part(v, bs):
                        for b in bs:
                            act.wait_ge(pt_mm, GB * v + b + 1)
                            copy(pt[:, b], PS[0:C, P_PT + b % 2, :].rearrange("c (h s) -> c h s", s=S), pt_ev)

                    def ot_ev_step(v):
                        for pp in range(2):
                            act.wait_ge(pv_mm, 2 * v + pp + 1)
                            copy(ot2[:, pp, :], PS[:, P_S + pp, :], ot_ev)

                    def acc_ev_step(n):
                        act.wait_ge(wo_mm, NQ * n)
                        act.activation(acc2_sb[:], PS[:, P_ACC, :], ACT.Identity, bias=bo_sb[:]).then_inc(acc2_ev, 1)

                    def ft_hi_step(n):
                        act.wait_ge(ft_mm, n)
                        copy(ft_hi[:], PS[:, P_MISC, :], fthi_done)

                    def group(g, first, last):
                        for q in range(NQ):
                            u = NQ * g + q
                            if not (last and q == NQ - 1):
                                if not (first and q == 0):
                                    act.wait_ge(s_mm, GB * u)
                                g_ev_part((q + 1) % NQ, QH * (u + 1), (0, 1))
                            if q == 1 and not first:
                                acc_ev_step(g)
                            if not (first and q < 2):
                                act.wait_ge(pt_mm, GB * (u - 1))
                            exp_part(q, u, (0, 1))
                            if not (last and q == NQ - 1):
                                g_ev_part((q + 1) % NQ, QH * (u + 1), (2, 3))
                            exp_part(q, u, (2, 3))
                            if q == 3 and not last:
                                act.wait_ge(ctn_ready, g + 2)
                                copy_over()
                            if q == 3 and not first:
                                ft_hi_step(g)

                            def v_turn(i):
                                n = 2 * u + 3 + i
                                if q == 0:
                                    v_ev(2 + i, 0, n)
                                elif q < 3:
                                    v_ev(2 * q - 2 + i, 1, n)
                                elif not last:
                                    v_ev(i, 0, n)

                            if q == 1 and not first:
                                act.wait_ge(pv_mm, 2 * NQ * g)
                            if q == 3:
                                act.wait_ge(pv_mm, 2 * (u - 1))
                            previous = not (first and q == 0)
                            if previous:
                                pt_ev_part(u - 1, (0, 1))
                            if q < 3:
                                v_turn(0)
                            if previous:
                                pt_ev_part(u - 1, (2, 3))
                            if q == 2 and not last:
                                ct_hi_step(m_use(g, first, last, 2, "ct"))
                            v_turn(1 if q < 3 else 0)
                            if previous:
                                ot_ev_step(u - 1)
                            if q == 3 and not last:
                                v_turn(1)

                    ct_hi_step(0)
                    act.wait_ge(ctn_ready, 1)
                    copy_over()
                    v_ev(0, 0, 1)
                    g_ev_part(0, 0, range(QH))
                    v_ev(1, 0, 2)
                    group(0, True, False)
                    with act.Fori(1, NG - 1) as g:
                        group(g, False, False)
                    group(NG - 1, False, True)
                    pt_ev_part(NQ * NG - 1, range(GB))
                    ot_ev_step(NQ * NG - 1)
                    acc_ev_step(NG)
                    ft_hi_step(NG)

                @block.vector
                def _(dve):
                    A2, B2 = 1.0 + EPS_LN, EPS_OUT * EPS_LN

                    def x_of(g):
                        return lambda k: X[:, g * GB + k, :]

                    def c_of(g):
                        return lambda k: CX[:, g * GB + k, :]

                    def factor_ctx(g, n):
                        norm_factor(dve, c_of(g), C, n, 1.0, EPS_LN)

                    def apply_ctx(g, n):
                        norm_apply(dve, c_of(g), cn, C, n, cn_ready)

                    def factor_lat(g, n):
                        norm_factor(dve, x_of(g), 128, n, A2, B2)

                    def apply_lat(g, n):
                        norm_apply(dve, x_of(g), ln_x, 128, n, lnx_ready)

                    def factor_ffn(g, n):
                        norm_factor(dve, x_of(g), 128, n, 1.0, EPS_OUT)

                    def apply_ffn(g, n):
                        norm_apply(dve, x_of(g), fn, 128, n, fn_ready)

                    def cy_step(n):
                        dve.wait_ge(ct_mm, n)
                        dve.tensor_scalar(cy[:], PS[:, P_MISC, 0:GC], lnc_w_sb[:], lnc_b_sb[:], ALU.mult, ALU.add)\
                           .then_inc(misc2, 1)

                    def ct_lo_step(n):
                        dve.wait_ge(cthi_done, n)
                        dve.tensor_tensor(ctn_lo[:], cy[:], ctn_hi[:].bitcast(F32), ALU.subtract).then_inc(ctn_ready, 1)

                    def lat_step(n):
                        dve.wait_ge(lt_mm, n)
                        dve.tensor_scalar(lat_t[:], PS[:, P_MISC, :], lnl_w_sb[:], lnl_b_sb[:], ALU.mult, ALU.add)\
                           .then_inc(misc2, 1)

                    def softmax(q, u):
                        flat = e[:, q % 2].rearrange("s b c -> s (b c)")
                        rows = flat.rearrange("s (r c) -> s r c", c=C)
                        dve.wait_ge(s_ev, GB * (u + 1))
                        dve.tensor_scalar(flat, flat, EXP_HI, EXP_LO, ALU.min, ALU.max).then_inc(clipped, 1)
                        dve.wait_ge(clipped, u + 1)
                        dve.reduce_sum(sums[:], rows, AX.X).then_inc(summed, 1)
                        dve.wait_ge(summed, u + 1)
                        dve.reciprocal(rsum[:, :, 0], sums[:]).then_inc(inverted, 1)
                        dve.wait_ge(inverted, u + 1)
                        dve.tensor_tensor(rows, rows, rsum[:].broadcast_to([128, GB * QH, C]), ALU.mult)\
                           .then_inc(p_ready, 1)

                    def residual(g, n):
                        dve.wait_ge(fin2_mm, n)
                        xs = X[:, bass.ts(g, GB), :]
                        dve.tensor_tensor(xs, PS[:, P_MISC, :].rearrange("s (b d) -> s b d", d=D), xs, ALU.add)\
                           .then_inc(misc2, 1)

                    def ft_lo_step(n):
                        dve.wait_ge(fthi_done, n)
                        dve.tensor_tensor(ft_lo[:], PS[:, P_MISC, :], ft_hi[:].bitcast(F32), ALU.subtract)\
                           .then_inc(misc2, 1)

                    def last_residual(g, n):
                        dve.wait_ge(ff_mm, n)
                        xs = X[:, bass.ts(g, GB), :]
                        dve.tensor_tensor(xs, PS[:, P_MISC, :].rearrange("s (b d) -> s b d", d=D), xs, ALU.add)\
                           .then_inc(misc2, 1)

                    def group(g, first, last):
                        for q in range(NQ):
                            u = NQ * g + q
                            n = 2 if first else 3 * g + 1
                            if q == 0:
                                lat_step(g + 1)
                                if not last:
                                    factor_ctx(g + 1, n)
                            if q == 1 and not last:
                                apply_ctx(g + 1, n)
                                factor_lat(g + 1, n + 1)
                            if q == 2 and not first:
                                residual(g - 1, g)
                            if q == 2 and not last:
                                apply_lat(g + 1, n + 1)
                            if q == 2 and not first:
                                dve.wait_ge(misc2, m_use(g, first, last, 1, "fin") + 1)
                                dve.memset(rsum[:, 0, :], 0.0)
                                factor_ffn(g - 1, n if last else n + 2)
                            if q == 2 and not last:
                                cy_step(g + 2)
                            if q == 3 and not first:
                                apply_ffn(g - 1, n if last else n + 2)
                                ft_lo_step(g)
                                last_residual(g - 1, g)
                            softmax(q, u)
                            if q == 2 and not last:
                                ct_lo_step(g + 2)

                    dve.wait_ge(ctx_loaded, 16)
                    factor_ctx(0, 0)
                    apply_ctx(0, 0)
                    factor_lat(0, 1)
                    cy_step(1)
                    apply_lat(0, 1)
                    ct_lo_step(1)
                    group(0, True, False)
                    with dve.Fori(1, NG - 1) as g:
                        group(g, False, False)
                    group(NG - 1, False, True)
                    residual(NG - 1, NG)
                    dve.wait_ge(misc2, M_END + 1)
                    factor_ffn(NG - 1, 3 * NG - 1)
                    apply_ffn(NG - 1, 3 * NG - 1)
                    ft_lo_step(NG)
                    last_residual(NG - 1, NG)


_INS = ['x', 'ctx_1024', 'L0_attn_Wq', 'L0_attn_Wk', 'L0_attn_Wv', 'L0_attn_Wo', 'L0_attn_proj', 'L0_xattn_ln_l_w',
        'L0_xattn_ln_l_b', 'L0_xattn_ln_c_w', 'L0_xattn_ln_c_b', 'L0_xattn_Wq', 'L0_xattn_Wkv', 'L0_xattn_Wo',
        'L0_xattn_bo', 'L0_ffn_weight']


def kernel(**inputs):
    import numpy as _np
    import concourse.bacc as _bacc
    from concourse import mybir as _mybir
    from concourse.bass_utils import run_bass_kernel_spmd as _run

    nc = _bacc.Bacc("TRN2", target_bir_lowering=False, num_devices=1)
    arrays, args = {}, []
    for name in _INS:
        a = _np.ascontiguousarray(inputs[name])
        arrays[f"in_{name}"] = a
        args.append(nc.dram_tensor(f"in_{name}", a.shape, _mybir.dt.from_np(a.dtype), kind="ExternalInput").ap())
    shape = inputs['x'].shape
    args.append(nc.dram_tensor("out_x", shape, _mybir.dt.float32, kind="ExternalOutput").ap())
    decoder_layer(nc, *args)
    r = _run(nc, [arrays], core_ids=[0])
    return r.results[0]["out_x"]
```

```python
import concourse.bass as bass
from concourse import mybir
from contextlib import ExitStack


def decoder_layer(nc, x, ctx_in, wq1, wk1, wv1, wo1, proj, lnl_w, lnl_b, lnc_w, lnc_b,
                  wq2, wkv2, wo2, bo2, w_ffn, out):
    F32 = mybir.dt.float32
    F32R = mybir.dt.float32r
    ALU = mybir.AluOpType
    ACT = mybir.ActivationFunctionType
    AX = mybir.AxisListType

    NB, S, D = x.shape
    C = ctx_in.shape[1]
    HD = proj.shape[0]
    NH = wq1.shape[1] // HD
    NP = NH // 2
    GB = 4
    NG = NB // GB
    W = GB * S
    GC = GB * C
    INNER = NH * HD
    HALF = INNER // 2
    QH = 4
    NQ = NH // QH
    QC = QH * C
    EPS_OUT = 1e-5
    EPS_LN = 1e-5
    EPS_DEN = 1e-6
    SCALE = float(HD) ** -0.5
    EXP_HI, EXP_LO = 59874.141715197817, 1.670170079024566e-05

    stack = ExitStack()
    with stack:
        def sb(name, shape, dt=F32):
            return stack.enter_context(nc.sbuf_tensor(name, shape, dt))

        def sem(name):
            return stack.enter_context(nc.semaphore(name))

        X = sb("X", [128, NB, D])
        CX = sb("CX", [C, NB, D])
        ident = sb("ident", [128, 128])
        causal = sb("causal", [128, 1, S])
        wv2_hi, wv2_lo = sb("wv2_hi", [D, INNER], F32R), sb("wv2_lo", [D, INNER], F32R)
        m_hi, m_lo = sb("m_hi", [D, NH, D], F32R), sb("m_lo", [D, NH, D], F32R)
        wo2_hi, wo2_lo = sb("wo2_hi", [128, NP * D], F32R), sb("wo2_lo", [128, NP * D], F32R)
        sign_t = sb("sign_t", [D, D], F32R)
        lnl_w_sb, lnl_b_sb = sb("lnl_w_sb", [D, 1]), sb("lnl_b_sb", [D, 1])
        lnc_w_sb, lnc_b_sb = sb("lnc_w_sb", [D, 1]), sb("lnc_b_sb", [D, 1])
        bo_sb = sb("bo_sb", [D, 1])

        st6 = sb("st6", [128, GB, 6])
        mean = sb("mean", [128, GB, 1])
        m_sum, m_dif = sb("m_sum", [128, GB]), sb("m_dif", [128, GB])
        sq_sum, sq_dif = sb("sq_sum", [128, GB]), sb("sq_dif", [128, GB])
        var_part = sb("var_part", [128, GB])
        r1 = sb("r1", [128, GB, 1])
        t1 = sb("t1", [128, GB, 1])
        minus_half = sb("minus_half", [128, 16])

        def variance(dve, parts, n, a, b, halves, done, mean, var):
            p = slice(0, parts)
            dve.tensor_tensor(m_sum[p], st6[p, :, 1], st6[p, :, 4], ALU.add)
            dve.tensor_tensor(m_dif[p], st6[p, :, 1], st6[p, :, 4], ALU.subtract)
            dve.tensor_tensor(sq_sum[p], st6[p, :, 2], st6[p, :, 5], ALU.add).then_inc(halves, 1)
            dve.wait_ge(halves, 2 * n + 1)
            dve.tensor_scalar(mean[p, :, 0], m_sum[p], 0.5, None, ALU.mult)
            dve.tensor_scalar(var_part[p], sq_sum[p], a / D, b, ALU.mult, ALU.add)
            dve.scalar_tensor_tensor(sq_dif[p], m_dif[p], a / 4, m_dif[p], ALU.mult, ALU.mult).then_inc(halves, 1)
            dve.wait_ge(halves, 2 * n + 2)
            dve.tensor_tensor(var[p, :, 0], var_part[p], sq_dif[p], ALU.add).then_inc(done, 1)

        xn = sb("xn", [128, GB, D])
        ln_st, ln_mv, ln_v = sem("ln_st"), sem("ln_mv"), sem("ln_v")
        ln_r, xn_ready = sem("ln_r"), sem("xn_ready")

        def ln_stats(dve, g, n):
            for b in range(GB):
                i = dve.bn_stats(st6[:, b, :], X[:, g * GB + b, :])
            i.then_inc(ln_st, 1)

        def ln_variance(dve, n):
            dve.wait_ge(ln_st, n + 1)
            variance(dve, 128, n, 1.0, EPS_OUT, ln_mv, ln_v, mean, t1)

        def ln_apply(dve, g, n):
            dve.wait_ge(ln_r, n + 1)
            for b in range(GB):
                i = dve.tensor_scalar(xn[:, b, :], X[:, g * GB + b, :], mean[:, b, :], r1[:, b, :],
                                      ALU.subtract, ALU.mult)
            i.then_inc(xn_ready, 1)

        def ln_power(pool, n):
            pool.wait_ge(ln_v, n + 1)
            pool.tensor_tensor(r1[:, :, 0], t1[:, :, 0], minus_half[:, 0:GB], ALU.pow).then_inc(ln_r, 1)

        cn = sb("b_cn", [C, GB, D])
        ln_x = sb("b_ln_x", [128, GB, D])
        st_done, mv_done = sem("st_done"), sem("mv_done")
        cn_ready, lnx_ready, fn_ready = sem("cn_ready"), sem("lnx_ready"), sem("fn_ready")

        class Norm:
            def __init__(self, name):
                self.mean = sb(f"b_mean_{name}", [128, GB, 1])
                self.var = sb(f"b_var_{name}", [128, GB, 1])
                self.factor = sb(f"b_factor_{name}", [128, GB, 1])
                self.var_done = sem(f"var_done_{name}")
                self.factor_done = sem(f"factor_done_{name}")
                self.centred = sem(f"centred_{name}")

        norm_ctx, norm_lat, norm_ffn = Norm("ctx"), Norm("lat"), Norm("ffn")

        def norm_factor(dve, norm, src, parts, n, a, b):
            for k in range(GB):
                i = dve.bn_stats(st6[0:parts, k, :], src(k))
            i.then_inc(st_done, 1)
            dve.wait_ge(st_done, n + 1)
            variance(dve, parts, n, a, b, mv_done, norm.var_done, norm.mean, norm.var)

        def factor_ctx(dve, g, n):
            norm_factor(dve, norm_ctx, lambda k: CX[:, g * GB + k, :], C, n, 1.0, EPS_LN)

        def factor_lat(dve, g, n):
            norm_factor(dve, norm_lat, lambda k: X[:, g * GB + k, :], 128, n, 1.0 + EPS_LN, EPS_OUT * EPS_LN)

        def factor_ffn(dve, g, n):
            norm_factor(dve, norm_ffn, lambda k: X[:, g * GB + k, :], 128, n, 1.0, EPS_OUT)

        def norm_power(pool, norm, g, parts=128):
            pool.wait_ge(norm.var_done, g + 1)
            p = slice(0, parts)
            pool.tensor_tensor(norm.factor[p, :, 0], norm.var[p, :, 0], minus_half[p, 0:GB], ALU.pow)\
                .then_inc(norm.factor_done, 1)

        def norm_apply(pool, norm, src, dst, parts, g, ready):
            norm_power(pool, norm, g, parts)
            p = slice(0, parts)
            pool.tensor_tensor(dst[p], src[p], norm.mean[p].broadcast_to([parts, GB, D]), ALU.subtract)\
                .then_inc(norm.centred, 1)
            pool.wait_ge(norm.factor_done, g + 1)
            pool.wait_ge(norm.centred, g + 1)
            pool.tensor_tensor(dst[p], dst[p], norm.factor[p].broadcast_to([parts, GB, D]), ALU.mult)\
                .then_inc(ready, 1)

        phase_a = stack.enter_context(ExitStack())

        def wsb(name):
            return phase_a.enter_context(nc.sbuf_tensor(name, [128, INNER], F32R))

        wq1_hi, wq1_lo = wsb("wq1_hi"), wsb("wq1_lo")
        wk1_hi, wk1_lo = wsb("wk1_hi"), wsb("wk1_lo")
        wv1_hi, wv1_lo = wsb("wv1_hi"), wsb("wv1_lo")
        wo1_hi, wo1_lo = wsb("wo1_hi"), wsb("wo1_lo")

        rawv2 = phase_a.enter_context(nc.sbuf_tensor("rawv2", [D, INNER], F32))
        rawo2 = phase_a.enter_context(nc.sbuf_tensor("rawo2", [128, NP * D], F32))
        ffn_t, ffn_gt, ffn_lt = (phase_a.enter_context(nc.sbuf_tensor(n, [D, D], F32)) for n in
                                 ("ffn_t", "ffn_gt", "ffn_lt"))

        PS = stack.enter_context(nc.psum_tensor("PS", [128, 8, 512], F32))

        w_in = {name: sem(f"{name}_in")
                for name in ("wq1", "wk1", "wv1", "wo1", "wq2", "wk2", "wv2", "wo2", "proj", "ffn")}
        small_in = sem("small_in")
        x_in = [sem(f"x_in{i}") for i in range(3)]
        ctx_loaded = sem("ctx_loaded")
        zeroed, consts = sem("zeroed"), sem("consts")
        t_mm, t_cp = sem("t_mm"), sem("t_cp")
        p_mm, p_hi, p_lo = sem("p_mm"), sem("p_hi"), sem("p_lo")
        s_hi, s_lo = sem("s_hi"), sem("s_lo")
        sign_done, sign_gt, sign_lt = sem("sign_done"), sem("sign_gt"), sem("sign_lt")
        x_cut = [0, GB, 4 * GB, NB] if NB > 4 * GB else [0, GB, 2 * GB, NB]

        split_b = ((w_in["wv2"], rawv2, wv2_hi, wv2_lo), (w_in["wo2"], rawo2, wo2_hi, wo2_lo))

        def high_split(act, matrices):
            for loaded, src, hi, _ in matrices:
                act.wait_ge(loaded, 16)
                act.activation(hi[:], src[:], ACT.Copy).then_inc(s_hi, 1)

        def low_split(dve, matrices, before):
            for i, (_, src, hi, lo) in enumerate(matrices):
                dve.wait_ge(s_hi, before + i + 1)
                dve.tensor_tensor(lo[:], src[:], hi[:].bitcast(F32), ALU.subtract).then_inc(s_lo, 1)

        prep_stack = ExitStack()
        with prep_stack:
            def psb(name, shape, dt=F32):
                return prep_stack.enter_context(nc.sbuf_tensor(name, shape, dt))

            raw = [psb(f"raw{i}", [D, INNER]) for i in range(4)]
            rawv1 = psb("rawv1", [D, INNER])
            rawo1 = psb("rawo1", [128, NP * D])
            wt = [psb(f"wt{i}", [128, INNER]) for i in range(4)]
            projbd = psb("projbd", [128, 128])
            ffn_raw = psb("ffn_raw", [D, D])
            NT = NP // 4
            NM = NH // 4
            T_BANKS = P_BANKS = 4
            raw_in = [w_in[name] for name in ("wq1", "wk1", "wq2", "wk2")]
            split_a = ((w_in["wv1"], rawv1, wv1_hi, wv1_lo), (w_in["wo1"], rawo1, wo1_hi, wo1_lo))
            dests = []
            for hi, lo in ((wq1_hi, wq1_lo), (wk1_hi, wk1_lo)):
                for c in range(0, NP, 4):
                    dests.append((hi[:, c * 128:(c + 4) * 128], lo[:, c * 128:(c + 4) * 128]))
            for c in range(0, NH, 4):
                h = (c // 8) * 8 + (c // 4) % 2
                dests.append((m_hi[:, h:h + 7:2, :], m_lo[:, h:h + 7:2, :]))

            with nc.Block() as block:

                @block.sync
                def _(sp):
                    def load_x(c):
                        sp.dma_start(X[:, x_cut[c]:x_cut[c + 1], :],
                                     x[x_cut[c]:x_cut[c + 1]].rearrange("b s d -> s b d")).then_inc(x_in[c], 16)

                    sp.dma_start(raw[0][:], wq1).then_inc(w_in["wq1"], 16)
                    sp.dma_start(raw[1][:], wk1).then_inc(w_in["wk1"], 16)
                    load_x(0)
                    sp.dma_start(raw[2][:], wq2).then_inc(w_in["wq2"], 16)
                    sp.dma_start(raw[3][:], wkv2[:, 0:INNER]).then_inc(w_in["wk2"], 16)
                    sp.dma_start(ffn_raw[:], w_ffn).then_inc(w_in["ffn"], 16)
                    load_x(1)
                    load_x(2)
                    sp.dma_start(rawv2[:], wkv2[:, INNER:2 * INNER]).then_inc(w_in["wv2"], 16)
                    sp.dma_start(rawo2[:].rearrange("r (p d) -> r p d", d=D),
                                  wo2.rearrange("(p r) d -> r p d", r=128)).then_inc(w_in["wo2"], 16)
                    for dst, src in ((lnl_w_sb, lnl_w), (lnl_b_sb, lnl_b), (lnc_w_sb, lnc_w), (lnc_b_sb, lnc_b),
                                     (bo_sb, bo2)):
                        sp.dma_start(dst[:], src.rearrange("(d o) -> d o", o=1)).then_inc(small_in, 16)
                    sp.dma_start(CX[:], ctx_in.rearrange("b c d -> c b d")).then_inc(ctx_loaded, 16)

                @block.gpsimd
                def _(pool):
                    pool.memset(projbd[:], 0.0).then_inc(zeroed, 1)
                    pool.memset(ident[:], 0.0).then_inc(zeroed, 1)
                    pool.memset(causal[:], 1.0).then_inc(zeroed, 1)
                    pool.memset(minus_half[:], -0.5).then_inc(zeroed, 1)
                    pool.wait_ge(zeroed, 4)
                    pool.affine_select(out=ident[:], in_=ident[:], compare_op=ALU.not_equal, fill=1.0,
                                       base=0, pattern=[[-1, 128]], channel_multiplier=1).then_inc(consts, 1)
                    pool.affine_select(out=causal[:, 0, :], in_=causal[:, 0, :], compare_op=ALU.is_ge, fill=0.0,
                                       base=0, pattern=[[1, S]], channel_multiplier=-1).then_inc(consts, 1)
                    ln_power(pool, 0)

                @block.tensor
                def _(pe):
                    def transposes(i):
                        pe.wait_ge(raw_in[i], 16)
                        for c in range(NT):
                            n = i * NT + c
                            if n >= T_BANKS:
                                pe.wait_ge(t_cp, n - T_BANKS + 1)
                            for k in range(4):
                                at = (4 * c + k) * 128
                                mm = pe.transpose(PS[:, n % T_BANKS, k * 128:(k + 1) * 128], raw[i][:, at:at + 128],
                                                  ident[:])
                            mm.then_inc(t_mm, 1)

                    def product_bank(n):
                        if n >= P_BANKS:
                            pe.wait_ge(p_lo, n - P_BANKS + 1)
                        return PS[:, T_BANKS + n % P_BANKS, :]

                    def with_proj(i):
                        pe.wait_ge(t_cp, (i + 1) * NT)
                        for c in range(NT):
                            b = product_bank(i * NT + c)
                            for k in range(4):
                                at = (4 * c + k) * 128
                                mm = pe.matmul(b[:, k * 128:(k + 1) * 128], wt[i][:, at:at + 128], projbd[:],
                                               start=True, stop=True)
                            mm.then_inc(p_mm, 1)

                    pe.wait_ge(consts, 2)
                    transposes(0)
                    transposes(1)
                    pe.wait_ge(w_in["proj"], 32)
                    with_proj(0)
                    with_proj(1)
                    transposes(2)
                    transposes(3)
                    pe.wait_ge(t_cp, 4 * NT)
                    for n in range(NM):
                        b = product_bank(2 * NT + n)
                        for k in range(4):
                            h = (n // 2) * 8 + n % 2 + 2 * k
                            r, at = HD * (h % 2), (h // 2) * 128
                            mm = pe.matmul(b[:, k * 128:(k + 1) * 128], wt[3][r:r + HD, at:at + 128],
                                           wt[2][r:r + HD, at:at + 128], start=True, stop=True)
                        mm.then_inc(p_mm, 1)
                    pe.wait_ge(w_in["ffn"], 16)
                    pe.transpose(PS[:, 0, 0:128], ffn_raw[:], ident[:]).then_inc(t_mm, 1)

                @block.scalar
                def _(act):
                    act.wait_ge(zeroed, 3)
                    act.dma_start(projbd[0:HD, 0:HD], proj).then_inc(w_in["proj"], 16)
                    act.dma_start(projbd[HD:128, HD:128], proj).then_inc(w_in["proj"], 16)
                    act.dma_start(rawv1[:], wv1).then_inc(w_in["wv1"], 16)
                    act.dma_start(rawo1[:].rearrange("r (p d) -> r p d", d=D),
                                  wo1.rearrange("(p r) d -> r p d", r=128)).then_inc(w_in["wo1"], 16)

                    def copy_transposes(i):
                        for c in range(NT):
                            n = i * NT + c
                            act.wait_ge(t_mm, n + 1)
                            act.activation(wt[i][:, c * 512:(c + 1) * 512], PS[:, n % T_BANKS, :], ACT.Copy)\
                               .then_inc(t_cp, 1)

                    def high_parts(ns):
                        for n in ns:
                            act.wait_ge(p_mm, n + 1)
                            act.activation(dests[n][0], PS[:, T_BANKS + n % P_BANKS, :], ACT.Copy).then_inc(p_hi, 1)

                    copy_transposes(0)
                    copy_transposes(1)
                    high_parts(range(2 * NT))
                    copy_transposes(2)
                    copy_transposes(3)
                    for i in range(2):
                        high_parts((2 * NT + i,))
                        high_split(act, split_a[i:i + 1])
                    high_parts(range(2 * NT + 2, len(dests)))
                    act.wait_ge(t_mm, 4 * NT + 1)
                    act.activation(ffn_t[:], PS[:, 0, 0:D], ACT.Copy).then_inc(t_cp, 1)

                @block.vector
                def _(dve):
                    def low_parts(ns):
                        for n in ns:
                            hi, lo = dests[n]
                            dve.wait_ge(p_hi, n + 1)
                            dve.tensor_tensor(lo, PS[:, T_BANKS + n % P_BANKS, :], hi.bitcast(F32), ALU.subtract)\
                               .then_inc(p_lo, 1)

                    low_parts(range(2 * NT))
                    dve.wait_ge(x_in[0], 16)
                    ln_stats(dve, 0, 0)
                    ln_variance(dve, 0)
                    for i in range(2):
                        low_parts((2 * NT + i,))
                        low_split(dve, split_a[i:i + 1], i)
                    ln_apply(dve, 0, 0)
                    low_parts(range(2 * NT + 2, len(dests)))

        with ExitStack() as pa:
            def asb(name, shape, dt=F32):
                return pa.enter_context(nc.sbuf_tensor(name, shape, dt))

            def asem(name):
                return pa.enter_context(nc.semaphore(name))

            xt_hi, xt_lo = asb("a_xt_hi", [D, W], F32R), asb("a_xt_lo", [D, W], F32R)
            xtn_hi, xtn_lo = asb("a_xtn_hi", [D, W], F32R), asb("a_xtn_lo", [D, W], F32R)
            e_q, e_k, r_k = asb("a_e_q", [128, W]), asb("a_e_k", [128, W]), asb("a_r_k", [128, W])
            fq, fk = asb("a_fq", [128, W]), asb("a_fk", [128, W])
            fq_hi, fq_lo = asb("a_fq_hi", [128, GB, 2, S], F32R), asb("a_fq_lo", [128, GB, 2, S], F32R)
            fk_hi, fk_lo = asb("a_fk_hi", [128, W], F32R), asb("a_fk_lo", [128, W], F32R)
            am = asb("a_am", [128, GB, 2, S])
            v = asb("a_v", [128, GB, NH, HD + 1])
            den = asb("a_den", [128, 2, GB, 1])
            rden = asb("a_rden", [128, 2, GB, 1])
            on = asb("a_on", [128, 2, GB, 2, HD])
            ot_hi, ot_lo = asb("a_ot_hi", [128, W], F32R), asb("a_ot_lo", [128, W], F32R)
            acc_sb = asb("a_acc_sb", [D, W])

            B_QK, B_MISC, B_A, B_O, B_OT, B_ACC = 0, 1, 2, 4, 6, 7

            q_proj, k_proj = asem("q_proj"), asem("k_proj")
            nq_done = asem("nq_done")
            eq_done, ek_done = asem("eq_done"), asem("ek_done")
            fq_done, fk_done = asem("fq_done"), asem("fk_done")
            fqhi_done, fqlo_done = asem("fqhi_done"), asem("fqlo_done")
            fkhi_done, fklo_done = asem("fkhi_done"), asem("fklo_done")
            a_done, mask_done = asem("a_done"), asem("mask_done")
            av_done, norm_done = asem("av_done"), asem("norm_done")
            den_done, rden_done = asem("den_done"), asem("rden_done")
            ot_done, wo_done = asem("ot_done"), asem("wo_done")
            othi_done, otlo_done = asem("othi_done"), asem("otlo_done")
            v_mm = asem("v_mm")
            misc_free = asem("misc_free")
            acc_evac, fin_done = asem("acc_evac"), asem("fin_done")
            xt_done, xthi_done, cur_ready = asem("xt_done"), asem("xthi_done"), asem("cur_ready")
            ones_set = asem("ones_set")

            N_PRO = 1 + GB

            def use(g, first, p, kind):
                i = p + (1 if p > 3 else 0)
                if kind == "xt":
                    i = 4
                if not first and (p > 1 or kind == "fin"):
                    i += 1
                return (N_PRO if first else 10 * g + 4) + (i if not (kind == "fin") else 2)

            def split3(pe, dst, w_hi, w_lo, x_hi, x_lo, start=True, stop=True):
                pe.matmul(dst, w_hi, x_hi, start=start, stop=False)
                pe.matmul(dst, w_hi, x_lo, start=False, stop=False)
                return pe.matmul(dst, w_lo, x_hi, start=False, stop=stop)

            def v_bank(b, i):
                return B_A + b if i is None else B_MISC

            def v_args(b, half, hi, lo):
                s, c = slice(b * S, (b + 1) * S), slice(half * HALF, (half + 1) * HALF)
                return hi[:, s], lo[:, s], wv1_hi[:, c], wv1_lo[:, c]

            with nc.Block() as block:

                @block.sync
                def _(sp):
                    sp.wait_ge(x_in[2], 16)
                    sp.wait_ge(small_in, 5 * 16)

                @block.tensor
                def _(pe):
                    def xt_transposes(g, i):
                        pe.wait_ge(xn_ready, g + 1)
                        if not (isinstance(i, int) and i == 0):
                            pe.wait_ge(misc_free, i)
                        for b in range(GB):
                            mm = pe.transpose(PS[:, B_MISC, b * S:(b + 1) * S], xn[:, b, :], ident[:])
                        mm.then_inc(xt_done, 1)

                    def v_half(b, half, hi, lo, i):
                        if i is not None:
                            pe.wait_ge(misc_free, i)
                        split3(pe, PS[:, v_bank(b, i), :], *v_args(b, half, hi, lo)).then_inc(v_mm, 1)

                    def proj_step(p, w_hi, w_lo, hi, lo, done):
                        c = slice(p * 128, (p + 1) * 128)
                        split3(pe, PS[:, B_QK, :], w_hi[:, c], w_lo[:, c], hi[:], lo[:]).then_inc(done, 1)

                    def wo_step(p):
                        c = slice(p * D, (p + 1) * D)
                        split3(pe, PS[:, B_ACC, :], wo1_hi[:, c], wo1_lo[:, c], ot_hi[:], ot_lo[:],
                               start=(p == 0), stop=(p == NP - 1)).then_inc(wo_done, 1)

                    def fin_transposes(i, n):
                        pe.wait_ge(acc_evac, n)
                        pe.wait_ge(misc_free, i)
                        for b in range(GB):
                            mm = pe.transpose(PS[:, B_MISC, b * S:(b + 1) * S], acc_sb[:, b * S:(b + 1) * S], ident[:])
                        mm.then_inc(fin_done, 1)

                    def ot_transposes(p, bs=range(GB)):
                        for b in bs:
                            mm = pe.transpose(PS[:, B_OT, b * S:(b + 1) * S],
                                              on[:, p % 2, b, :, :].rearrange("s h d -> s (h d)"), ident[:])
                        if bs[-1] == GB - 1:
                            mm.then_inc(ot_done, 1)

                    def group(g, first, last):
                        for p in range(NP):
                            u = NP * g + p
                            begin = first and p == 0
                            more = not (last and p == NP - 1)
                            nxt = (p + 1) % NP
                            hi, lo = (xt_hi, xt_lo) if 3 <= p < NP - 1 else (xtn_hi, xtn_lo)
                            if p == 3:
                                pe.wait_ge(cur_ready, 2 * g + 2)
                            if more:
                                if p == NP - 1:
                                    pe.wait_ge(misc_free, use(g, first, 3, "xt") + 1)
                                pe.wait_ge(ek_done, u + 1)
                                proj_step(nxt, wq1_hi, wq1_lo, hi, lo, q_proj)
                            if p < GB:
                                v_half(p, 1, hi, lo, use(g, first, p, "v"))
                            elif not last:
                                v_half(p - GB, 0, xtn_hi, xtn_lo, use(g, first, p, "v"))
                            if not (first and p < 2):
                                pe.wait_ge(otlo_done, u - 1)
                                if p == 2 and not first:
                                    pe.wait_ge(acc_evac, g)
                                wo_step((p - 2) % NP)
                            pe.wait_ge(fqlo_done, 2 * u + 2)
                            pe.wait_ge(fklo_done, u + 1)
                            if begin:
                                pe.wait_ge(misc_free, N_PRO)
                            else:
                                pe.wait_ge(mask_done, 2 * u)
                            for b in range(GB):
                                c = slice(b * S, (b + 1) * S)
                                mm = split3(pe, PS[:, B_A + b // 2, (b % 2) * 2 * S:(b % 2 + 1) * 2 * S],
                                            fk_hi[:, c], fk_lo[:, c], fq_hi[:, b].rearrange("p h s -> p (h s)"),
                                            fq_lo[:, b].rearrange("p h s -> p (h s)"))
                                if b % 2 == 1:
                                    mm.then_inc(a_done, 1)
                            if p == 3 and not last:
                                xt_transposes(g + 1, use(g, first, 3, "xt"))
                            if not begin:
                                pe.wait_ge(norm_done, u)
                                ot_transposes((p - 1) % NP, (0, 1))
                            if more:
                                pe.wait_ge(fq_done, u + 2)
                                proj_step(nxt, wk1_hi, wk1_lo, hi, lo, k_proj)
                            if not begin:
                                ot_transposes((p - 1) % NP, (2, 3))
                            if p == 1 and not first:
                                fin_transposes(use(g, first, 1, "fin"), g)
                            if p == 0:
                                pe.wait_ge(misc_free, use(g, first, 0, "v"))
                            if p == GB:
                                pe.wait_ge(misc_free, use(g, first, 3, "v") + 1)
                            for b in range(GB):
                                if b % 2 == 0:
                                    pe.wait_ge(mask_done, 2 * u + 1 + b // 2)
                                for h in range(2):
                                    mm = pe.matmul(PS[:, B_O + h, b * (HD + 1):(b + 1) * (HD + 1)],
                                                   am[:, b, h, :], v[:, b, 2 * p + h, :], start=True, stop=True)
                            mm.then_inc(av_done, 1)

                    xt_transposes(0, 0)
                    pe.wait_ge(misc_free, 1)
                    proj_step(0, wq1_hi, wq1_lo, xtn_hi, xtn_lo, q_proj)
                    v_half(0, 0, xtn_hi, xtn_lo, None)
                    v_half(1, 0, xtn_hi, xtn_lo, None)
                    pe.wait_ge(fq_done, 1)
                    proj_step(0, wk1_hi, wk1_lo, xtn_hi, xtn_lo, k_proj)
                    v_half(2, 0, xtn_hi, xtn_lo, None)
                    v_half(3, 0, xtn_hi, xtn_lo, None)
                    group(0, True, False)
                    with pe.Fori(1, NG - 1) as g:
                        group(g, False, False)
                    group(NG - 1, False, True)
                    U = NP * NG
                    pe.wait_ge(otlo_done, U - 1)
                    wo_step(NP - 2)
                    pe.wait_ge(norm_done, U)
                    ot_transposes(NP - 1)
                    pe.wait_ge(otlo_done, U)
                    wo_step(NP - 1)
                    fin_transposes(use(NG - 1, False, 3, "v") + 1, NG)

                @block.scalar
                def _(act):
                    def exp_q_step(u1, read):
                        act.wait_ge(q_proj, u1)
                        if read is not None:
                            act.wait_ge(fq_done, read)
                        act.activation(e_q[:], PS[:, B_QK, :], ACT.Relu, scale=-1.0).then_inc(nq_done, 1)
                        act.wait_ge(nq_done, u1)
                        act.activation(e_q[:], e_q[:], ACT.Exp, scale=-1.0).then_inc(eq_done, 1)

                    def exp_k_step(u1, read):
                        act.wait_ge(k_proj, u1)
                        if read is not None:
                            act.wait_ge(fk_done, read)
                        act.activation(r_k[:], PS[:, B_QK, :], ACT.Relu)
                        act.activation(e_k[:], PS[:, B_QK, :], ACT.Exp).then_inc(ek_done, 1)

                    def v_evac(b, half, n, bank=B_MISC):
                        act.wait_ge(v_mm, n)
                        act.activation(v[:, b, half * NP:(half + 1) * NP, 0:HD],
                                       PS[:, bank, :].rearrange("s (h d) -> s h d", d=HD),
                                       ACT.Copy).then_inc(misc_free, 1)

                    def ot_hi_step(n):
                        act.wait_ge(ot_done, n)
                        act.activation(ot_hi[:], PS[:, B_OT, :], ACT.Copy).then_inc(othi_done, 1)

                    def xt_hi_evac(n):
                        act.wait_ge(xt_done, n)
                        act.activation(xtn_hi[:], PS[:, B_MISC, :], ACT.Copy).then_inc(xthi_done, 1)

                    def copy_over(part):
                        dst, src = ((xt_hi, xtn_hi), (xt_lo, xtn_lo))[part]
                        act.activation(dst[:], src[:].bitcast(F32), ACT.Copy).then_inc(cur_ready, 1)

                    def acc_to_sbuf(n):
                        act.wait_ge(wo_done, NP * n)
                        act.activation(acc_sb[:], PS[:, B_ACC, :], ACT.Copy).then_inc(acc_evac, 1)

                    def v_turn(g, p, first, last):
                        u = NP * g + p
                        if p < GB:
                            if not first:
                                act.wait_ge(av_done, NP * g)
                            v_evac(p, 1, u + GB + 1)
                        elif not last:
                            act.wait_ge(av_done, u - p + NP // 2)
                            v_evac(p - GB, 0, u + GB + 1)

                    def fq_hi_step(u):
                        act.wait_ge(fq_done, u + 1)
                        for h in range(2):
                            r = slice(h * HD, (h + 1) * HD)
                            act.activation(fq_hi[r, :, h, :], fq[r].rearrange("p (b s) -> p b s", s=S), ACT.Copy)\
                               .then_inc(fqhi_done, 1)

                    def fk_hi_step(u):
                        act.wait_ge(fk_done, u + 1)
                        act.activation(fk_hi[:], fk[:], ACT.Copy).then_inc(fkhi_done, 1)

                    def group(g, first, last):
                        for p in range(NP):
                            u = NP * g + p
                            begin = first and p == 0
                            more = not (last and p == NP - 1)
                            if not begin:
                                act.wait_ge(a_done, 2 * u)
                            fk_hi_step(u)
                            if more:
                                exp_q_step(u + 2, u + 1)
                            v_turn(g, p, first, last)
                            if p == 1 and not first:
                                acc_to_sbuf(g)
                            if p in (0, 2):
                                copy_over(p // 2)
                            if more:
                                act.wait_ge(a_done, 2 * u + 2)
                                fq_hi_step(u + 1)
                            if p == 3 and not last:
                                xt_hi_evac(g + 2)
                            if more:
                                exp_k_step(u + 2, u + 1)
                            if first and p in (5, 6):
                                high_split(act, split_b[p - 5:p - 4])
                            if not begin:
                                if not (first and p == 1):
                                    act.wait_ge(wo_done, u - 1)
                                ot_hi_step(u)

                    xt_hi_evac(1)
                    exp_q_step(1, None)
                    act.wait_ge(ones_set, 3)
                    fq_hi_step(0)
                    v_evac(0, 0, 1, v_bank(0, None))
                    v_evac(1, 0, 2, v_bank(1, None))
                    exp_k_step(1, None)
                    v_evac(2, 0, 3, v_bank(2, None))
                    v_evac(3, 0, 4, v_bank(3, None))
                    group(0, True, False)
                    with act.Fori(1, NG - 1) as g:
                        group(g, False, False)
                    group(NG - 1, False, True)
                    act.wait_ge(wo_done, NP * NG - 1)
                    ot_hi_step(NP * NG)
                    acc_to_sbuf(NG)

                @block.gpsimd
                def _(pool):
                    pool.memset(v[:, :, :, HD:HD + 1], 1.0).then_inc(ones_set, 1)
                    pool.memset(fq_hi[:].bitcast(F32), 0.0).then_inc(ones_set, 1)
                    pool.memset(fq_lo[:].bitcast(F32), 0.0).then_inc(ones_set, 1)
                    pool.wait_ge(ones_set, 3)

                    def fq_lo_step(u):
                        for h in range(2):
                            r = slice(h * HD, (h + 1) * HD)
                            pool.wait_ge(fqhi_done, 2 * u + h + 1)
                            pool.tensor_tensor(fq_lo[r, :, h, :], fq[r].rearrange("p (b s) -> p b s", s=S),
                                               fq_hi[r, :, h, :].bitcast(F32), ALU.subtract).then_inc(fqlo_done, 1)
                            pool.wait_ge(fqlo_done, 2 * u + h + 1)

                    def group(g, last):
                        for p in range(NP):
                            if not (last and p == NP - 1):
                                fq_lo_step(NP * g + p + 1)
                            if p == 1 and not last:
                                ln_power(pool, g + 1)

                    fq_lo_step(0)
                    group(0, False)
                    with pool.Fori(1, NG - 1) as g:
                        group(g, False)
                    group(NG - 1, True)
                    norm_apply(pool, norm_ctx, CX[:, 0:GB, :], cn, C, 0, cn_ready)
                    norm_apply(pool, norm_lat, X[:, 0:GB, :], ln_x, 128, 0, lnx_ready)

                @block.vector
                def _(dve):
                    def feature_q(u1):
                        dve.wait_ge(eq_done, u1)
                        dve.scalar_tensor_tensor(fq[:], PS[:, B_QK, :], 0.0, e_q[:], ALU.max, ALU.add)\
                           .then_inc(fq_done, 1)

                    def feature_k(u1):
                        dve.wait_ge(ek_done, u1)
                        dve.scalar_tensor_tensor(fk[:], e_k[:], 1.0, r_k[:], ALU.min, ALU.add).then_inc(fk_done, 1)

                    def fk_lo_step(u):
                        dve.wait_ge(fkhi_done, u + 1)
                        dve.tensor_tensor(fk_lo[:], fk[:], fk_hi[:].bitcast(F32), ALU.subtract).then_inc(fklo_done, 1)

                    def mask(j, u):
                        dve.wait_ge(a_done, 2 * u + j + 1)
                        dve.tensor_tensor(am[:, 2 * j:2 * j + 2].rearrange("k b h s -> k (b h) s"),
                                          PS[:, B_A + j, :].rearrange("k (c s) -> k c s", s=S),
                                          causal[:].broadcast_to([128, 4, S]), ALU.mult).then_inc(mask_done, 1)

                    def normalise(p, n, wait_ot):
                        dve.wait_ge(av_done, n)
                        o = PS[:, B_O:B_O + 2, 0:GB * (HD + 1)].rearrange("s h (b e) -> s h b e", e=HD + 1)
                        dve.tensor_scalar(den[:, :, :, 0], o[:, :, :, HD], EPS_DEN, None, ALU.add).then_inc(den_done, 1)
                        dve.wait_ge(den_done, n)
                        dve.reciprocal(rden[:], den[:]).then_inc(rden_done, 1)
                        dve.wait_ge(rden_done, n)
                        if wait_ot is not None:
                            dve.wait_ge(ot_done, wait_ot)
                        dve.tensor_tensor(on[:, p % 2].rearrange("s b h d -> s h b d"), o[:, :, :, 0:HD],
                                          rden[:].broadcast_to([128, 2, GB, HD]), ALU.mult).then_inc(norm_done, 1)

                    def ot_lo_step(n):
                        dve.wait_ge(othi_done, n)
                        dve.tensor_tensor(ot_lo[:], PS[:, B_OT, :], ot_hi[:].bitcast(F32), ALU.subtract)\
                           .then_inc(otlo_done, 1)

                    def xt_lo_evac(n):
                        dve.wait_ge(xthi_done, n)
                        dve.tensor_tensor(xtn_lo[:], PS[:, B_MISC, :], xtn_hi[:].bitcast(F32), ALU.subtract)\
                           .then_inc(misc_free, 1)

                    def residual(g, n):
                        dve.wait_ge(fin_done, n)
                        xs = X[:, bass.ts(g, GB), :]
                        dve.tensor_tensor(xs, PS[:, B_MISC, :].rearrange("s (b d) -> s b d", d=D), xs, ALU.add)\
                           .then_inc(misc_free, 1)

                    def signs():
                        dve.wait_ge(t_cp, 4 * NP // 4 + 1)
                        dve.tensor_scalar(ffn_gt[:], ffn_t[:], 0.0, None, ALU.is_gt).then_inc(sign_gt, 1)
                        dve.tensor_scalar(ffn_lt[:], ffn_t[:], 0.0, None, ALU.is_lt).then_inc(sign_lt, 1)
                        dve.wait_ge(sign_gt, 1)
                        dve.wait_ge(sign_lt, 1)
                        dve.tensor_tensor(sign_t[:], ffn_gt[:], ffn_lt[:], ALU.subtract).then_inc(sign_done, 1)

                    def group(g, first, last):
                        for p in range(NP):
                            u = NP * g + p
                            begin = first and p == 0
                            more = not (last and p == NP - 1)
                            if not (first and p < 2):
                                ot_lo_step(u - 1)
                            fk_lo_step(u)
                            if not begin:
                                normalise((p - 1) % NP, u, None if first and p < 3 else u - 2)
                            if more:
                                dve.wait_ge(fqlo_done, 2 * u + 2)
                                feature_q(u + 2)
                            mask(0, u)
                            mask(1, u)
                            if p == 0 and not last:
                                if first:
                                    dve.wait_ge(x_in[1], 16)
                                ln_stats(dve, g + 1, g + 1)
                            if p == 1 and not first:
                                residual(g - 1, g)
                            if p == 1 and not last:
                                ln_variance(dve, g + 1)
                            if p == 2 and not last:
                                ln_apply(dve, g + 1, g + 1)
                            if p == 3 and not last:
                                xt_lo_evac(g + 2)
                            if last and p == 1:
                                dve.wait_ge(ctx_loaded, 16)
                                factor_ctx(dve, 0, 0)
                            if last and p == 3:
                                factor_lat(dve, 0, 1)
                            if more:
                                feature_k(u + 2)
                            if first and p in (6, 7):
                                low_split(dve, split_b[p - 6:p - 5], 2 + p - 6)
                            if first and p == 5:
                                signs()

                    xt_lo_evac(1)
                    dve.wait_ge(ones_set, 1)
                    feature_q(1)
                    feature_k(1)
                    group(0, True, False)
                    dve.wait_ge(x_in[2], 16)
                    with dve.Fori(1, NG - 1) as g:
                        group(g, False, False)
                    group(NG - 1, False, True)
                    ot_lo_step(NP * NG - 1)
                    normalise(NP - 1, NP * NG, NP * NG - 2)
                    ot_lo_step(NP * NG)
                    residual(NG - 1, NG)

        phase_a.close()

        with ExitStack() as pb:
            def bsb(name, shape, dt=F32):
                return pb.enter_context(nc.sbuf_tensor(name, shape, dt))

            def bsem(name):
                return pb.enter_context(nc.semaphore(name))

            cy = bsb("b_cy", [D, GC])
            ct_hi, ct_lo = bsb("b_ct_hi", [D, GC], F32R), bsb("b_ct_lo", [D, GC], F32R)
            ctn_hi, ctn_lo = bsb("b_ctn_hi", [D, GC], F32R), bsb("b_ctn_lo", [D, GC], F32R)
            lat_t = bsb("b_lat_t", [D, W])
            lat_hi, lat_lo = bsb("b_lat_hi", [D, W], F32R), bsb("b_lat_lo", [D, W], F32R)
            g_hi = bsb("b_g_hi", [D, 2, GB, QC], F32R)
            g_lo = bsb("b_g_lo", [D, 2, GB, QC], F32R)
            e = bsb("b_e", [128, 2, GB, QC])
            sums = bsb("b_sums", [128, GB * QH])
            rsum = bsb("b_rsum", [128, GB * QH, 1])
            pt = bsb("b_pt", [C, GB, QH, S])
            v2 = bsb("b_v2", [C, GB, NH, HD])
            ot2_hi, ot2_lo = bsb("b_ot_hi", [128, 2, W], F32R), bsb("b_ot_lo", [128, 2, W], F32R)
            acc2_sb = bsb("b_acc_sb", [D, W])
            fn = bsb("b_fn", [128, GB, D])
            ft_hi, ft_lo = bsb("b_ft_hi", [D, W], F32R), bsb("b_ft_lo", [D, W], F32R)

            P_ACC, P_G, P_S, P_PT, P_MISC = 0, 1, 3, 5, 7
            P_VB, P_TB = P_PT, P_PT + 1

            g_mm, ghi_done, g_ev = bsem("g_mm"), bsem("ghi_done"), bsem("g_ev")
            s_mm, s_ev = bsem("s_mm"), bsem("s_ev")
            clipped, summed, inverted, p_ready = bsem("clipped"), bsem("summed"), bsem("inverted"), bsem("p_ready")
            pt_mm, pt_ev = bsem("pt_mm"), bsem("pt_ev")
            pv_mm, othi2, ot_ev = bsem("pv_mm"), bsem("othi2"), bsem("ot_ev")
            wo_mm = bsem("wo_mm")
            lathi_done, lat_done = bsem("lathi_done"), bsem("lat_done")
            v2_mm = bsem("v2_mm")
            vb_ev = bsem("vb_ev")
            res_done = bsem("res_done")
            latt_done = bsem("latt_done")
            misc2 = bsem("misc2")
            acc2_ev, fin2_mm = bsem("acc2_ev"), bsem("fin2_mm")
            ct_mm, cthi_done, ctn_ready, ct_cur = bsem("ct_mm"), bsem("cthi_done"), bsem("ctn_ready"), bsem("ct_cur")
            lt_mm = bsem("lt_mm")
            ft_mm, fthi_done, ff_mm = bsem("ft_mm"), bsem("fthi_done"), bsem("ff_mm")
            x_out = bsem("x_out")

            M_PRO = 3

            def m_use(g, first, last, kind):
                order = ["v0", "v1"] + ([] if last else ["ct"]) + ["v2"] + ([] if first else ["ft", "ff"]) + ["v3"]
                return (M_PRO if first else 7 * g + 1) + order.index(kind)

            M_END = 7 * (NG - 1) + 6

            with nc.Block() as block:

                @block.sync
                def _(sp):
                    def store(g, i):
                        sp.wait_ge(misc2, i + 1)
                        sp.dma_start(out[bass.ts(g, GB)].rearrange("b s d -> s b d"), X[:, bass.ts(g, GB), :])\
                          .then_inc(x_out, 16)

                    with sp.Fori(0, NG - 2) as g:
                        store(g, 7 * g + m_use(1, False, False, "ff"))
                    store(NG - 2, m_use(NG - 1, False, True, "ff"))
                    store(NG - 1, M_END + 1)
                    sp.wait_ge(x_out, 16 * NG)

                @block.gpsimd
                def _(pool):
                    def apply_ctx(g):
                        pool.wait_ge(ct_mm, g)
                        norm_apply(pool, norm_ctx, CX[:, bass.ts(g, GB), :], cn, C, g, cn_ready)

                    def apply_lat(g):
                        pool.wait_ge(lt_mm, g)
                        norm_apply(pool, norm_lat, X[:, bass.ts(g, GB), :], ln_x, 128, g, lnx_ready)

                    def divide(u, q):
                        rows = e[:, q % 2].rearrange("s b (h c) -> s (b h) c", c=C)
                        pool.wait_ge(inverted, u + 1)
                        pool.tensor_tensor(rows, rows, rsum[:].broadcast_to([128, GB * QH, C]), ALU.mult)\
                            .then_inc(p_ready, 1)

                    def group(g, first, last):
                        for q in range(NQ):
                            if q == 1 and not last:
                                apply_ctx(g + 1)
                            if q == 2 and not last:
                                apply_lat(g + 1)
                            if q == 3 and not first:
                                norm_power(pool, norm_ffn, g - 1)
                            divide(NQ * g + q, q)

                    group(0, True, False)
                    with pool.Fori(1, NG - 1) as g:
                        group(g, False, False)
                    group(NG - 1, False, True)
                    norm_power(pool, norm_ffn, NG - 1)

                @block.tensor
                def _(pe):
                    def three(dst, w_hi, w_lo, x_hi, x_lo, start=True, stop=True):
                        pe.matmul(dst, w_hi, x_hi, start=start, stop=False)
                        pe.matmul(dst, w_hi, x_lo, start=False, stop=False)
                        return pe.matmul(dst, w_lo, x_hi, start=False, stop=stop)

                    def g_heads(q, heads, hi, lo, base):
                        for i in heads:
                            h = QH * q + i
                            if not (isinstance(base, int) and base + i < 2):
                                pe.wait_ge(g_ev, base + i - 1)
                            three(PS[:, P_G + i % 2, 0:GC], m_hi[:, h, :], m_lo[:, h, :], hi[:], lo[:]).then_inc(g_mm, 1)

                    def v_step(b, half, hi, lo, i):
                        if i is not None:
                            pe.wait_ge(misc2, i)
                        s, c = slice(b * C, (b + 1) * C), slice(half * HALF, (half + 1) * HALF)
                        three(PS[0:C, P_VB if i is None else P_MISC, :], hi[:, s], lo[:, s], wv2_hi[:, c], wv2_lo[:, c]).then_inc(v2_mm, 1)

                    def four_transposes(bank, src, done):
                        for b in range(GB):
                            mm = pe.transpose(PS[:, bank, b * S:(b + 1) * S], src(b), ident[:])
                        mm.then_inc(done, 1)

                    def ct_transposes(n, i):
                        pe.wait_ge(cn_ready, n)
                        if i is not None:
                            pe.wait_ge(misc2, i)
                        for b in range(GB):
                            mm = pe.transpose(PS[:, P_MISC, b * C:(b + 1) * C], cn[:, b, :], ident[0:C, 0:C])
                        mm.then_inc(ct_mm, 1)

                    def lt_transposes(n):
                        pe.wait_ge(lnx_ready, n)
                        four_transposes(P_TB, lambda b: ln_x[:, b, :], lt_mm)

                    def fin_transposes(n):
                        pe.wait_ge(acc2_ev, n)
                        four_transposes(P_TB, lambda b: acc2_sb[:, b * S:(b + 1) * S], fin2_mm)

                    def ft_transposes(n, i):
                        pe.wait_ge(fn_ready, n)
                        pe.wait_ge(misc2, i)
                        four_transposes(P_MISC, lambda b: fn[:, b, :], ft_mm)

                    def ffn(i_ft, i):
                        pe.wait_ge(misc2, i_ft + 1)
                        pe.wait_ge(misc2, i)
                        for b in range(GB):
                            s = slice(b * S, (b + 1) * S)
                            pe.matmul(PS[:, P_MISC, s], ft_hi[:, s], sign_t[:], start=True, stop=False)
                            mm = pe.matmul(PS[:, P_MISC, s], ft_lo[:, s], sign_t[:], start=False, stop=True)
                        mm.then_inc(ff_mm, 1)

                    def wo_step(q, n):
                        for pp in range(2):
                            pe.wait_ge(ot_ev, 2 * (n - 1) + pp + 1)
                            k = 2 * q + pp
                            mm = three(PS[:, P_ACC, :], wo2_hi[:, k * D:(k + 1) * D], wo2_lo[:, k * D:(k + 1) * D], ot2_hi[:, pp, :],
                                       ot2_lo[:, pp, :], start=(k == 0), stop=(k == NP - 1))
                        mm.then_inc(wo_mm, 1)

                    def scores(q, u, bs, begin):
                        pe.wait_ge(g_ev, QH * (u + 1))
                        for b in bs:
                            if b < 2 and not begin:
                                pe.wait_ge(ot_ev, 2 * (u - 2) + b + 1)
                            elif b >= 2 or not (isinstance(u, int) and u == 0):
                                pe.wait_ge(s_ev, GB * u + b - 1)
                            s = slice(b * S, (b + 1) * S)
                            three(PS[:, P_S + b % 2, 0:QC], lat_hi[:, s], lat_lo[:, s], g_hi[:, q % 2, b, :],
                                  g_lo[:, q % 2, b, :]).then_inc(s_mm, 1)

                    def pt_part(q, v, bs, begin):
                        pe.wait_ge(p_ready, v + 1)
                        for b in bs:
                            if not (begin and b < 2):
                                pe.wait_ge(pt_ev, GB * v + b - 1)
                            for i in range(QH):
                                mm = pe.transpose(PS[0:C, P_PT + b % 2, i * S:(i + 1) * S],
                                                  e[:, q % 2, b, i * C:(i + 1) * C], ident[:])
                            mm.then_inc(pt_mm, 1)

                    def pv_part(q, v, bs):
                        pe.wait_ge(pt_ev, GB * v + bs[-1] + 1)
                        for pp in range(2):
                            for b in bs:
                                for i in range(2):
                                    mm = pe.matmul(PS[i * HD:(i + 1) * HD, P_S + pp, b * S:(b + 1) * S],
                                                   v2[:, b, QH * q + 2 * pp + i, :], pt[:, b, 2 * pp + i, :],
                                                   start=True, stop=True)
                            if bs[-1] == GB - 1:
                                mm.then_inc(pv_mm, 1)

                    def group(g, first, last):
                        for q in range(NQ):
                            u = NQ * g + q
                            more = not (last and q == NQ - 1)

                            def at(kind):
                                return m_use(g, first, last, kind)
                            hi, lo = (ctn_hi, ctn_lo) if q == NQ - 1 else (ct_hi, ct_lo)
                            if more:
                                if q == 0:
                                    pe.wait_ge(ct_cur, g + 1)
                                if q == NQ - 1:
                                    pe.wait_ge(ctn_ready, g + 2)
                                g_heads((q + 1) % NQ, (0, 1), hi, lo, QH * (u + 1))
                            if not (first and q < 2):
                                if q == 2 and not first:
                                    pe.wait_ge(acc2_ev, g)
                                wo_step((q - 2) % NQ, u - 1)
                            if q == 0:
                                pe.wait_ge(lat_done, g + 1)
                            scores(q, u, (0, 1), first and q < 2)
                            if more:
                                g_heads((q + 1) % NQ, (2, 3), hi, lo, QH * (u + 1))
                            scores(q, u, (2, 3), first and q < 2)
                            if q == 2 and not last:
                                ct_transposes(g + 2, at("ct"))
                            def v_turn(i):
                                use = at(f"v{q}") if i == q // 3 else None
                                if q == 0:
                                    v_step(2 + i, 0, ct_hi, ct_lo, use)
                                elif q < 3:
                                    v_step(2 * q - 2 + i, 1, ct_hi, ct_lo, use)
                                elif not last:
                                    v_step(i, 0, ctn_hi, ctn_lo, use)

                            previous = not (first and q == 0)
                            if previous:
                                pe.wait_ge(vb_ev, u)
                                if q == 2 and not first:
                                    pe.wait_ge(res_done, g)
                                pt_part((q - 1) % NQ, u - 1, (0, 1), first and q == 1)
                            if q == 3 and not first:
                                ft_transposes(g, at("ft"))
                            if q < 3:
                                v_turn(0)
                            if previous:
                                pt_part((q - 1) % NQ, u - 1, (2, 3), first and q == 1)
                                if q == 1:
                                    pe.wait_ge(misc2, at("v0") + 1)
                                if q == 3:
                                    pe.wait_ge(misc2, at("v2") + 1)
                                pe.wait_ge(s_ev, GB * (u + 1))
                                pv_part((q - 1) % NQ, u - 1, (0, 1))
                            if q == 3 and not first:
                                ffn(at("ft"), at("ff"))
                            if previous:
                                pv_part((q - 1) % NQ, u - 1, (2, 3))
                            if q == 3 and not last:
                                v_turn(0)
                                lt_transposes(g + 2)
                            v_turn(1)
                            if q == 1 and not first:
                                fin_transposes(g)

                    pe.wait_ge(consts, 2)
                    ct_transposes(1, None)
                    pe.wait_ge(ctn_ready, 1)
                    v_step(0, 0, ctn_hi, ctn_lo, 1)
                    g_heads(0, range(QH), ctn_hi, ctn_lo, 0)
                    v_step(1, 0, ctn_hi, ctn_lo, 2)
                    lt_transposes(1)
                    group(0, True, False)
                    with pe.Fori(1, NG - 1) as g:
                        group(g, False, False)
                    group(NG - 1, False, True)
                    U = NQ * NG
                    wo_step(NQ - 2, U - 1)
                    pt_part(NQ - 1, U - 1, range(GB), False)
                    pv_part(NQ - 1, U - 1, range(GB))
                    wo_step(NQ - 1, U)
                    fin_transposes(NG)
                    ft_transposes(NG, M_END)
                    ffn(M_END, M_END + 1)

                @block.scalar
                def _(act):
                    def copy(dst, src, done):
                        act.activation(dst, src, ACT.Copy).then_inc(done, 1)

                    def cy_step(n):
                        act.wait_ge(ct_mm, n)
                        act.activation(cy[:], PS[:, P_MISC, 0:GC], ACT.Identity, scale=lnc_w_sb[:], bias=lnc_b_sb[:])\
                           .then_inc(misc2, 1)

                    def ct_hi_step(i):
                        act.wait_ge(misc2, i + 1)
                        copy(ctn_hi[:], cy[:], cthi_done)

                    def lat_step(n):
                        act.wait_ge(lt_mm, n)
                        act.activation(lat_t[:], PS[:, P_TB, :], ACT.Identity, scale=lnl_w_sb[:], bias=lnl_b_sb[:])\
                           .then_inc(latt_done, 1)

                    def copy_over():
                        act.activation(ct_hi[:], ctn_hi[:].bitcast(F32), ACT.Copy)
                        copy(ct_lo[:], ctn_lo[:].bitcast(F32), ct_cur)

                    def v_ev(b, half, n, bank, done):
                        act.wait_ge(v2_mm, n)
                        copy(v2[:, b, half * NP:(half + 1) * NP, :],
                             PS[0:C, bank, :].rearrange("c (h d) -> c h d", d=HD), done)

                    def exp_part(q, u, bs):
                        for b in bs:
                            act.wait_ge(s_mm, GB * u + b + 1)
                            act.activation(e[:, q % 2, b, :], PS[:, P_S + b % 2, 0:QC], ACT.Exp, scale=SCALE)\
                               .then_inc(s_ev, 1)

                    def g_ev_part(q, base, heads):
                        for i in heads:
                            act.wait_ge(g_mm, base + i + 1)
                            copy(g_hi[:, q % 2, :, i * C:(i + 1) * C],
                                 PS[:, P_G + i % 2, 0:GC].rearrange("p (b c) -> p b c", c=C), ghi_done)

                    def pt_ev_part(v, bs):
                        for b in bs:
                            act.wait_ge(pt_mm, GB * v + b + 1)
                            copy(pt[:, b], PS[0:C, P_PT + b % 2, :].rearrange("c (h s) -> c h s", s=S), pt_ev)

                    def ot_ev_step(v):
                        for pp in range(2):
                            act.wait_ge(pv_mm, 2 * v + pp + 1)
                            copy(ot2_hi[:, pp, :], PS[:, P_S + pp, :], othi2)

                    def lat_hi_step(n):
                        act.wait_ge(latt_done, n)
                        copy(lat_hi[:], lat_t[:], lathi_done)

                    def acc_ev_step(n):
                        act.wait_ge(wo_mm, NQ * n)
                        act.activation(acc2_sb[:], PS[:, P_ACC, :], ACT.Identity, bias=bo_sb[:]).then_inc(acc2_ev, 1)

                    def ft_hi_step(n):
                        act.wait_ge(ft_mm, n)
                        copy(ft_hi[:], PS[:, P_MISC, :], fthi_done)

                    def group(g, first, last):
                        for q in range(NQ):
                            u = NQ * g + q
                            if not (last and q == NQ - 1):
                                if not (first and q == 0):
                                    act.wait_ge(s_mm, GB * u)
                                g_ev_part((q + 1) % NQ, QH * (u + 1), (0, 1))
                            if q == 1 and not first:
                                acc_ev_step(g)
                            if not (first and q < 2):
                                act.wait_ge(pt_mm, GB * (u - 1))
                            exp_part(q, u, (0, 1))
                            if not (last and q == NQ - 1):
                                g_ev_part((q + 1) % NQ, QH * (u + 1), (2, 3))
                            exp_part(q, u, (2, 3))
                            def v_turn(i):
                                n = 2 * u + 3 + i
                                to = (P_MISC, misc2) if i == q // 3 else (P_VB, vb_ev)
                                if q == 0:
                                    v_ev(2 + i, 0, n, *to)
                                elif q < 3:
                                    v_ev(2 * q - 2 + i, 1, n, *to)
                                elif not last:
                                    v_ev(i, 0, n, *to)

                            if q == 1 and not first:
                                act.wait_ge(pv_mm, 2 * NQ * g)
                            if q == 3:
                                act.wait_ge(pv_mm, 2 * (u - 1))
                            previous = not (first and q == 0)
                            if q == 2 and not last:
                                cy_step(g + 2)
                            if previous:
                                pt_ev_part(u - 1, (0, 1))
                            if q == 3 and not first:
                                ft_hi_step(g)
                            if q < 3:
                                v_turn(0)
                            if previous:
                                pt_ev_part(u - 1, (2, 3))
                            if q == 2 and not last:
                                ct_hi_step(m_use(g, first, last, "ct"))
                            if q == 3 and not last:
                                act.wait_ge(ctn_ready, g + 2)
                                copy_over()
                            if previous:
                                ot_ev_step(u - 1)
                            if q == 3 and not last:
                                v_turn(0)
                                lat_step(g + 2)
                                lat_hi_step(g + 2)
                            v_turn(1)

                    cy_step(1)
                    ct_hi_step(0)
                    act.wait_ge(ctn_ready, 1)
                    copy_over()
                    v_ev(0, 0, 1, P_MISC, misc2)
                    g_ev_part(0, 0, range(QH))
                    v_ev(1, 0, 2, P_MISC, misc2)
                    lat_step(1)
                    lat_hi_step(1)
                    group(0, True, False)
                    with act.Fori(1, NG - 1) as g:
                        group(g, False, False)
                    group(NG - 1, False, True)
                    pt_ev_part(NQ * NG - 1, range(GB))
                    ot_ev_step(NQ * NG - 1)
                    acc_ev_step(NG)
                    ft_hi_step(NG)

                @block.vector
                def _(dve):
                    def apply_ffn(g):
                        dve.wait_ge(norm_ffn.factor_done, g + 1)
                        for k in range(GB):
                            i = dve.tensor_scalar(fn[:, k, :], X[:, g * GB + k, :], norm_ffn.mean[:, k, :],
                                                  norm_ffn.factor[:, k, :], ALU.subtract, ALU.mult)
                        i.then_inc(fn_ready, 1)

                    def ct_lo_step(n):
                        dve.wait_ge(cthi_done, n)
                        dve.tensor_tensor(ctn_lo[:], cy[:], ctn_hi[:].bitcast(F32), ALU.subtract).then_inc(ctn_ready, 1)

                    def lat_lo_step(n):
                        dve.wait_ge(lathi_done, n)
                        dve.tensor_tensor(lat_lo[:], lat_t[:], lat_hi[:].bitcast(F32), ALU.subtract)\
                           .then_inc(lat_done, 1)

                    def g_lo_part(q, base, heads):
                        for i in heads:
                            dve.wait_ge(ghi_done, base + i + 1)
                            c = slice(i * C, (i + 1) * C)
                            dve.tensor_tensor(g_lo[:, q % 2, :, c],
                                              PS[:, P_G + i % 2, 0:GC].rearrange("p (b c) -> p b c", c=C),
                                              g_hi[:, q % 2, :, c].bitcast(F32), ALU.subtract).then_inc(g_ev, 1)

                    def ot_lo_step(v):
                        for pp in range(2):
                            dve.wait_ge(othi2, 2 * v + pp + 1)
                            dve.tensor_tensor(ot2_lo[:, pp, :], PS[:, P_S + pp, :], ot2_hi[:, pp, :].bitcast(F32),
                                              ALU.subtract).then_inc(ot_ev, 1)

                    def exp_sums(u, q):
                        flat = e[:, q % 2].rearrange("s b c -> s (b c)")
                        rows = flat.rearrange("s (r c) -> s r c", c=C)
                        dve.wait_ge(s_ev, GB * (u + 1))
                        dve.tensor_scalar(flat, flat, EXP_HI, EXP_LO, ALU.min, ALU.max).then_inc(clipped, 1)
                        dve.wait_ge(clipped, u + 1)
                        dve.reduce_sum(sums[:], rows, AX.X).then_inc(summed, 1)

                        dve.wait_ge(summed, u + 1)
                        if not (isinstance(u, int) and u == 0):
                            dve.wait_ge(p_ready, u)
                        dve.reciprocal(rsum[:, :, 0], sums[:]).then_inc(inverted, 1)

                    def residual(g, n):
                        dve.wait_ge(fin2_mm, n)
                        xs = X[:, bass.ts(g, GB), :]
                        dve.tensor_tensor(xs, PS[:, P_TB, :].rearrange("s (b d) -> s b d", d=D), xs, ALU.add)\
                           .then_inc(res_done, 1)

                    def ft_lo_step(n):
                        dve.wait_ge(fthi_done, n)
                        dve.tensor_tensor(ft_lo[:], PS[:, P_MISC, :], ft_hi[:].bitcast(F32), ALU.subtract)\
                           .then_inc(misc2, 1)

                    def last_residual(g, n):
                        dve.wait_ge(ff_mm, n)
                        xs = X[:, bass.ts(g, GB), :]
                        dve.tensor_tensor(xs, PS[:, P_MISC, :].rearrange("s (b d) -> s b d", d=D), xs, ALU.add)\
                           .then_inc(misc2, 1)

                    def group(g, first, last):
                        for q in range(NQ):
                            u = NQ * g + q
                            n = 2 if first else 3 * g + 1
                            more = not (last and q == NQ - 1)
                            if q == 0:
                                lat_lo_step(g + 1)
                            if q == 2 and not first:
                                residual(g - 1, g)
                            if more:
                                g_lo_part((q + 1) % NQ, QH * (u + 1), (0, 1))
                            if q == 0 and not last:
                                factor_ctx(dve, g + 1, n)
                            if q == 1 and not last:
                                factor_lat(dve, g + 1, n + 1)
                            if q == 2 and not first:
                                dve.wait_ge(res_done, g)
                                dve.memset(sums[:, 0:1], 0.0)
                                factor_ffn(dve, g - 1, n if last else n + 2)
                            if q == 3 and not first:
                                apply_ffn(g - 1)
                            if more:
                                g_lo_part((q + 1) % NQ, QH * (u + 1), (2, 3))
                            if q == 3 and not first:
                                ft_lo_step(g)
                            exp_sums(u, q)
                            if q == 2 and not last:
                                ct_lo_step(g + 2)
                            if q == 3 and not first:
                                last_residual(g - 1, g)
                            if not (first and q == 0):
                                ot_lo_step(u - 1)

                    ct_lo_step(1)
                    g_lo_part(0, 0, range(QH))
                    group(0, True, False)
                    with dve.Fori(1, NG - 1) as g:
                        group(g, False, False)
                    group(NG - 1, False, True)
                    ot_lo_step(NQ * NG - 1)
                    residual(NG - 1, NG)
                    dve.wait_ge(res_done, NG)
                    factor_ffn(dve, NG - 1, 3 * NG - 1)
                    apply_ffn(NG - 1)
                    ft_lo_step(NG)
                    last_residual(NG - 1, NG)


_INS = ['x', 'ctx_1024', 'L0_attn_Wq', 'L0_attn_Wk', 'L0_attn_Wv', 'L0_attn_Wo', 'L0_attn_proj', 'L0_xattn_ln_l_w',
        'L0_xattn_ln_l_b', 'L0_xattn_ln_c_w', 'L0_xattn_ln_c_b', 'L0_xattn_Wq', 'L0_xattn_Wkv', 'L0_xattn_Wo',
        'L0_xattn_bo', 'L0_ffn_weight']


def kernel(**inputs):
    import numpy as _np
    import concourse.bacc as _bacc
    from concourse import mybir as _mybir
    from concourse.bass_utils import run_bass_kernel_spmd as _run

    nc = _bacc.Bacc("TRN2", target_bir_lowering=False, num_devices=1)
    arrays, args = {}, []
    for name in _INS:
        a = _np.ascontiguousarray(inputs[name])
        arrays[f"in_{name}"] = a
        args.append(nc.dram_tensor(f"in_{name}", a.shape, _mybir.dt.from_np(a.dtype), kind="ExternalInput").ap())
    shape = inputs['x'].shape
    args.append(nc.dram_tensor("out_x", shape, _mybir.dt.float32, kind="ExternalOutput").ap())
    decoder_layer(nc, *args)
    r = _run(nc, [arrays], core_ids=[0])
    return r.results[0]["out_x"]
```
